# Optimizing a Trainium2 kernel written in Bass

```python
import numpy as np
import jax
import jax.numpy as jnp

def _softmax(x, axis=-1):
    return jax.nn.softmax(x, axis=axis)

def _gelu(x):
    return jax.nn.gelu(x, approximate=True)

def _silu(x):
    return jax.nn.silu(x)

def _sigmoid(x):
    return jax.nn.sigmoid(x)

def _layernorm(x, axis=-1, eps=1e-05):
    m = jnp.mean(x, axis=axis, keepdims=True)
    v = jnp.var(x, axis=axis, keepdims=True)
    return (x - m) / jnp.sqrt(v + eps)

def _scatter_add(tgt, idx, src, axis=0):
    return tgt.at[idx].add(src)

def _segment_sum(src, seg, n):
    return jax.ops.segment_sum(src, seg, n)
kernel_name = 'mk_gnn_preln_d1_gnn_r8_2a8192'

def setup_inputs(seed: int=0):
    np.random.seed(seed)
    _w = jnp.asarray

    def _rec_inputs():
        import jax
        import jax.numpy as jnp
        _gk = jax.random.key(seed)
        x = -0.0003713 + 1 * jax.random.normal(jax.random.fold_in(_gk, 1), (12500, 256), jnp.float32)
        src = jax.random.randint(jax.random.fold_in(_gk, 2), (200000,), 0, 12500, jnp.int32)
        dst = jax.random.randint(jax.random.fold_in(_gk, 3), (200000,), 0, 12500, jnp.int32)
        _o = jnp.argsort(dst, stable=True)
        src = src[_o]
        dst = dst[_o]
        edge_attr_32 = 0.000216709 + 1.00012 * jax.random.normal(jax.random.fold_in(_gk, 11), (200000, 32), jnp.float32)
        return (x, src, dst, edge_attr_32)
    x, src, dst, edge_attr_32 = _rec_inputs()

    def _L0_gnn_setup():
        import jax, jax.numpy as jnp
        import numpy as np
        N, E, D, H, C = (6250, 100000, 256, 4, 64)

        def _gat_layer(h_in, W, a_s, a_d, b, src, dst, n):
            Hh, Cc = a_s.shape
            h = (h_in @ W).reshape(n, Hh, Cc)
            alpha_s = jnp.sum(h * a_s, axis=-1)
            alpha_d = jnp.sum(h * a_d, axis=-1)
            e = jax.nn.leaky_relu(alpha_s[src] + alpha_d[dst], 0.2)
            m = jax.lax.stop_gradient(jax.ops.segment_max(e, dst, num_segments=n))
            ex = jnp.exp(e - m[dst])
            alpha = ex / jax.ops.segment_sum(ex, dst, num_segments=n)[dst]
            out = jax.ops.segment_sum(h[src] * alpha[:, :, None], dst, num_segments=n)
            return out.reshape(n, Hh * Cc) + b
        key = jax.random.key(seed)
        ks = jax.random.split(key, 12)
        x = jax.random.normal(ks[0], (N, D), dtype=jnp.float32)
        src = jax.random.randint(ks[1], (E,), 0, N, dtype=jnp.int32)
        dst = jax.random.randint(ks[2], (E,), 0, N, dtype=jnp.int32)
        dst = jnp.where(dst == src, (dst + 1) % N, dst)
        edge_index = jnp.stack([src, dst], axis=0)
        edge_attr = jax.random.normal(ks[3], (E, 32), dtype=jnp.float32)
        s = 1.0 / np.sqrt(D)
        sc = 1.0 / np.sqrt(C)
        return {'x': x, 'edge_index': edge_index, 'edge_attr': edge_attr, 'W0': jax.random.normal(ks[4], (D, H * C), dtype=jnp.float32) * s, 'a_src0': jax.random.normal(ks[5], (H, C), dtype=jnp.float32) * sc, 'a_dst0': jax.random.normal(ks[6], (H, C), dtype=jnp.float32) * sc, 'b0': jnp.zeros((H * C,), dtype=jnp.float32), 'W1': jax.random.normal(ks[7], (H * C, H * C), dtype=jnp.float32) * s, 'a_src1': jax.random.normal(ks[8], (H, C), dtype=jnp.float32) * sc, 'a_dst1': jax.random.normal(ks[9], (H, C), dtype=jnp.float32) * sc, 'b1': jnp.zeros((H * C,), dtype=jnp.float32)}
    _L0_gnn_all = _L0_gnn_setup()
    _L0_gnn_in = {k: v for k, v in _L0_gnn_all.items() if k in ('W0', 'a_src0', 'a_dst0', 'b0', 'W1', 'a_src1', 'a_dst1', 'b1')}
    del _L0_gnn_all
    return {'x': x, 'src': src, 'dst': dst, 'edge_attr_32': edge_attr_32, 'L0_gnn_W0': _L0_gnn_in['W0'], 'L0_gnn_a_src0': _L0_gnn_in['a_src0'], 'L0_gnn_a_dst0': _L0_gnn_in['a_dst0'], 'L0_gnn_b0': _L0_gnn_in['b0'], 'L0_gnn_W1': _L0_gnn_in['W1'], 'L0_gnn_a_src1': _L0_gnn_in['a_src1'], 'L0_gnn_a_dst1': _L0_gnn_in['a_dst1'], 'L0_gnn_b1': _L0_gnn_in['b1']}

def reference(x, src, dst, edge_attr_32, L0_gnn_W0, L0_gnn_a_src0, L0_gnn_a_dst0, L0_gnn_b0, L0_gnn_W1, L0_gnn_a_src1, L0_gnn_a_dst1, L0_gnn_b1):
    import jax
    import jax.numpy as jnp

    def _L0_gnn_ref(x, edge_index, edge_attr, W0, a_src0, a_dst0, b0, W1, a_src1, a_dst1, b1):
        import jax, jax.numpy as jnp
        import numpy as np
        N, E, D, H, C = (6250, 100000, 256, 4, 64)

        def _gat_layer(h_in, W, a_s, a_d, b, src, dst, n):
            Hh, Cc = a_s.shape
            h = (h_in @ W).reshape(n, Hh, Cc)
            alpha_s = jnp.sum(h * a_s, axis=-1)
            alpha_d = jnp.sum(h * a_d, axis=-1)
            e = jax.nn.leaky_relu(alpha_s[src] + alpha_d[dst], 0.2)
            m = jax.lax.stop_gradient(jax.ops.segment_max(e, dst, num_segments=n))
            ex = jnp.exp(e - m[dst])
            alpha = ex / jax.ops.segment_sum(ex, dst, num_segments=n)[dst]
            out = jax.ops.segment_sum(h[src] * alpha[:, :, None], dst, num_segments=n)
            return out.reshape(n, Hh * Cc) + b
        n = x.shape[0]
        loops = jnp.arange(n, dtype=edge_index.dtype)
        src = jnp.concatenate([edge_index[0], loops])
        dst = jnp.concatenate([edge_index[1], loops])
        h = jax.nn.gelu(_gat_layer(x, W0, a_src0, a_dst0, b0, src, dst, n), approximate=False)
        h = jax.nn.gelu(_gat_layer(h, W1, a_src1, a_dst1, b1, src, dst, n), approximate=False)
        return h
    edge_index = jnp.stack([src, dst])
    h = jnp.maximum(_layernorm(x, axis=-1), 0.0)
    x = x + _L0_gnn_ref(h, edge_index, edge_attr_32, L0_gnn_W0, L0_gnn_a_src0, L0_gnn_a_dst0, L0_gnn_b0, L0_gnn_W1, L0_gnn_a_src1, L0_gnn_a_dst1, L0_gnn_b1)
    return x

_drawn_inputs = setup_inputs


def setup_inputs(seed=0):
    import zlib

    import numpy as np

    out = dict(_drawn_inputs(seed))
    spreads = {'L0_gnn_b0': (0.0, 0.1), 'L0_gnn_b1': (0.0, 0.1)}
    factors = {'L0_gnn_a_src0': 5.079,
     'L0_gnn_a_dst0': 8.0,
     'L0_gnn_a_src1': 8.0,
     'L0_gnn_a_dst1': 22.601}
    for name, (base, spread) in spreads.items():
        noise = np.random.default_rng([zlib.crc32(name.encode()), seed]).standard_normal(out[name].shape)
        drawn = base * np.exp(spread * noise) if base else spread * noise
        out[name] = jnp.asarray(drawn.astype(out[name].dtype))
    for name, factor in factors.items():
        out[name] = (out[name] * factor).astype(out[name].dtype)
    return out
```

```python
from contextlib import ExitStack

import concourse.bass as bass
from concourse import mybir

ALU = mybir.AluOpType
ACT = mybir.ActivationFunctionType
AX = mybir.AxisListType
F32 = mybir.dt.float32
BF16 = mybir.dt.bfloat16
I32 = mybir.dt.int32

P = 128
BIG = 1.0e30


def wide(ap, axis, n):
    shape = list(ap.shape)
    return ap.unsqueeze(axis).broadcast_to(shape[:axis] + [n] + shape[axis:])


def two_layer_graph_attention(nc, x, src, dst, edge_attr, W0, a_src0, a_dst0, b0, W1, a_src1, a_dst1, b1, out):
    N, D = x.shape
    E = src.shape[0]
    H, C = a_src0.shape
    HC = H * C
    ROW = HC + 2 * H
    KC = D // P

    NT = 125
    TILES = N // NT
    PAIRS = TILES // 2
    IN_RUN = E // TILES // P + 1
    SLOTS = IN_RUN + 1
    CHUNK = SLOTS * P
    MAIN = IN_RUN * P
    HALF = IN_RUN // 2
    STRIDE = 16
    EP = 125
    EW = E // EP
    SAMPLES = EW // STRIDE
    PAD = CHUNK + P
    assert N % (2 * NT) == 0 and E % (EP * STRIDE) == 0 and D == HC and KC == 2 and IN_RUN == 16

    GROUP = 4
    GROUPS = N // (GROUP * P)
    REST = N - GROUPS * GROUP * P
    DPAIRS = GROUPS // 2
    assert GROUPS % 2 == 0 and P < REST <= 2 * P

    with ExitStack() as ctx:
        def sb(name, shape, dt=F32):
            return ctx.enter_context(nc.sbuf_tensor(name, shape, dt))

        def sem(name):
            return ctx.enter_context(nc.semaphore(name))

        def dram(name, shape, dt):
            return nc.dram_tensor(name, shape, dt, kind="Internal").ap()

        table = [dram("table0", [N, ROW], F32), dram("table1", [N, ROW], F32)]
        src_pad = dram("src_pad", [E + PAD], I32)
        dst_pad = dram("dst_pad", [E + PAD], I32)

        bank = [ctx.enter_context(nc.psum_tensor(f"bank{i}", [P, 512], F32)) for i in range(8)]

        ident = sb("ident", [P, P])
        ones = sb("ones", [P, P])
        iota_i = sb("iota_i", [P, P], I32)
        iota_f = sb("iota_f", [P, P])
        base_i = sb("base_i", [P, TILES + 1], I32)
        base_f = sb("base_f", [P, TILES + 1])
        eps = sb("eps", [P, 1])
        w_in = sb("w_in", [P, 2, KC, D])
        w_t = sb("w_t", [P, 2, KC, D])
        a_blk = sb("a_blk", [P, 2, KC, 2 * H])
        w_ext = sb("w_ext", [P, 2, KC, ROW])
        b_row = sb("b_row", [1, 2, HC])
        b_all = sb("b_all", [P, 2, HC])
        pad_i = sb("pad_i", [P, 2, PAD // P], I32)

        dst_all = sb("dst_all", [EP, EW], I32)
        samp = sb("samp", [EP, SAMPLES])
        below = sb("below", [EP, TILES + 1, SAMPLES], BF16)
        count = sb("count", [EP, TILES + 1])
        rank = sb("rank", [P, TILES + 1])
        start_f = sb("start_f", [P, TILES])
        last_f = sb("last_f", [P, TILES])
        last_i = sb("last_i", [P, TILES], I32)
        full_i = sb("full_i", [P, TILES], I32)
        full_f = sb("full_f", [P, TILES])
        chunks_f = sb("chunks_f", [P, 2, TILES])
        more_f = sb("more_f", [P, TILES])
        used_f = sb("used_f", [P, 2, TILES])
        cum_f = sb("cum_f", [P, 2 * TILES])
        cump_f = sb("cump_f", [P, 2, 2 * PAIRS])
        T_START, T_CHUNKS, T_MORE, T_BEFORE, T_BEFORE2, T_MORE2 = range(6)
        tiles_i = sb("tiles_i", [P, 6, 2 * TILES], I32)

        xg = [sb(f"xg{b}", [P, GROUP, D]) for b in range(2)]
        hn = [sb(f"hn{b}", [P, GROUP, D]) for b in range(2)]
        stats = [sb(f"stats{b}", [P, GROUP, 6]) for b in range(2)]
        mv = [sb(f"mv{b}", [P, GROUP, 2]) for b in range(2)]
        sdev = [sb(f"sdev{b}", [P, GROUP]) for b in range(2)]
        rstd = [sb(f"rstd{b}", [P, GROUP]) for b in range(2)]
        shift = [sb(f"shift{b}", [P, GROUP]) for b in range(2)]
        hnT = [sb(f"hnT{b}", [P, KC, P]) for b in range(2)]
        row0 = [sb(f"row0{b}", [P, GROUP, ROW]) for b in range(2)]

        src_i = [sb(f"src_i{b}", [P, SLOTS], I32) for b in range(2)]
        dst_i = [sb(f"dst_i{b}", [P, SLOTS], I32) for b in range(2)]
        self_row = [sb(f"self_row{b}", [NT, ROW]) for b in range(2)]
        x_row = [sb(f"x_row{b}", [NT, D]) for b in range(2)]
        G = [sb(f"G{b}", [P, SLOTS, ROW]) for b in range(2)]
        dloc = sb("dloc", [P, SLOTS])
        onehot = sb("onehot", [P, SLOTS, NT])
        onehotT = sb("onehotT", [NT, SLOTS, P])
        ends = sb("ends", [P, IN_RUN - 1])
        reset = sb("reset", [P, H, IN_RUN])
        away = sb("away", [P, 2, NT])
        a_run = sb("a_run", [P, H, IN_RUN])
        run_max = sb("run_max", [P, H, IN_RUN])
        marked = sb("marked", [P, IN_RUN - 1, H + 1])
        spread = sb("spread", [P, 2, H, NT])
        absent = sb("absent", [NT, IN_RUN - 1])
        seg = sb("seg", [NT, H, IN_RUN - 1])
        cands = sb("cands", [NT, H, 4])
        maxes = sb("maxes", [NT, 2, H])
        summed = sb("summed", [NT, 2, H])
        logit = sb("logit", [NT, 3, H])
        fall = sb("fall", [NT, H])
        scale = sb("scale", [NT, H])
        state = sb("state", [NT, HC + H])
        scaled = sb("scaled", [NT, HC + H])
        ye = sb("ye", [P, SLOTS, H])
        ze = sb("ze", [P, SLOTS, H])
        de = sb("de", [P, SLOTS, H])
        ce = sb("ce", [P, SLOTS, H])
        inv = sb("inv", [NT, H])
        mean_o = sb("mean_o", [NT, HC])
        o = sb("o", [NT, HC])
        act_o = sb("act_o", [NT, HC])
        act_oT = sb("act_oT", [P, KC, NT])
        row1 = sb("row1", [NT, ROW])
        y_out = sb("y_out", [NT, D])

        const_ready = sem("const_ready")
        w_landed, a_landed = sem("w_landed"), sem("a_landed")
        dst_landed = sem("dst_landed")
        wT_done, wT_copied, wa_done, w_ext_ready = sem("wT_done"), sem("wT_copied"), sem("wa_done"), sem("w_ext_ready")
        b_done = sem("b_done")
        prep_step = sem("prep_step")
        count_ready, rank_done, tiles_ready = sem("count_ready"), sem("rank_done"), sem("tiles_ready")
        gathers_begun, aggr_begun, loads_begun = sem("gathers_begun"), sem("aggr_begun"), sem("loads_begun")
        x_landed = [sem(f"x_landed{b}") for b in range(2)]
        stats_done = [sem(f"stats_done{b}") for b in range(2)]
        mv_done = [sem(f"mv_done{b}") for b in range(2)]
        sdev_done = [sem(f"sdev_done{b}") for b in range(2)]
        rstd_done = [sem(f"rstd_done{b}") for b in range(2)]
        shift_done = [sem(f"shift_done{b}") for b in range(2)]
        normed = [sem(f"normed{b}") for b in range(2)]
        hnT_done = [sem(f"hnT_done{b}") for b in range(2)]
        hnT_copied = [sem(f"hnT_copied{b}") for b in range(2)]
        rows_done = [sem(f"rows_done{b}") for b in range(2)]
        rows_copied = [sem(f"rows_copied{b}") for b in range(2)]
        rows_stored = [sem(f"rows_stored{b}") for b in range(2)]

        names = ("onehot_ready ends_ready away_ready run_ready max_ready marked_ready runs_done "
                 "spread_ready spreadT_done absent_ready seg_ready runmax_done cands_ready newmax_done sum_ready "
                 "logit_ready fall_ready scale_ready edge_done z_ready d_ready c_ready w_ready "
                 "scaled_ready state_moved state_set misc_set "
                 "inv_ready mean_ready o_ready act_ready actT_done actT_copied row_done row_copied y_ready_out").split()
        pairs = ("idx_landed self_landed x2_landed lo_landed hi_landed more_landed summed_up onehotT_done "
                 "onehotT_copied stored loc_done dst_read gathered").split()
        s = {**{n: sem(n) for n in names}, **{n: [sem(f"{n}{b}") for b in range(2)] for n in pairs},
             "part_weighted": [sem(f"part_weighted{k}") for k in range(3)]}

        from_one = [normed, hnT_done, rows_done, hnT_copied, rows_copied] + [s[n] for n in (
            "loc_done summed_up edge_done spreadT_done mean_ready actT_done y_ready_out row_done row_copied "
            "onehotT_copied state_moved act_ready dst_read gathered").split()]

        block = ctx.enter_context(nc.Block())

        def group_rows(ap, q, size):
            return ap[bass.ds(q * (GROUP * P), size * P), :].rearrange("(t p) c -> p t c", p=P)

        WHOLE, LAST = [P] * GROUP, [P, REST - P]

        @block.sync
        def _(sp):
            sp.dma_start(dst_all[:], dst.rearrange("(p w) -> p w", p=EP)).then_inc(dst_landed, 16)
            for one in from_one:
                for each in (one if isinstance(one, list) else [one]):
                    nc.sync.sem_inc(each, 1)
            for L, W in enumerate((W0, W1)):
                sp.dma_start(w_in[:, L], W.rearrange("(k p) c -> p k c", p=P)).then_inc(w_landed, 16)

            def load_group(q, i, b, sizes):
                sp.wait_ge(normed[b], i * GROUP + 1)
                if sizes is WHOLE:
                    sp.dma_start(xg[b][:], group_rows(x, q, GROUP)).then_inc(x_landed[b], 16)
                else:
                    r = GROUPS * GROUP * P
                    sp.dma_start(xg[b][:, 0, :], x[r:r + P, :]).then_inc(x_landed[b], 16)
                    sp.dma_start(xg[b][0:sizes[1], 1, :], x[r + P:N, :]).then_inc(x_landed[b], 16)

            with nc.sync.Fori(0, DPAIRS) as i:
                for b in range(2):
                    load_group(i * 2 + b, i, b, WHOLE)
            load_group(GROUPS, DPAIRS, 0, LAST)

            for L in range(2):
                if L == 0:
                    sp.wait_ge(tiles_ready, 1)
                    for b in range(2):
                        sp.wait_ge(s["stored"][b], 16)
                    sp.wait_ge(rows_stored[0], 16 * (DPAIRS + 3))
                    sp.wait_ge(rows_stored[1], 16 * (DPAIRS + 1))
                else:
                    for b in range(2):
                        sp.wait_ge(s["stored"][b], 16 * PAIRS + 16)
                with nc.sync.Fori(0, PAIRS) as i:
                    for b in range(2):
                        n = i * 2 + b
                        nn = n + L * TILES
                        start = sp.value_load(tiles_i[0:1, T_START, bass.ds(nn, 1)], min_val=0, max_val=E)
                        chunks = sp.value_load(tiles_i[0:1, T_CHUNKS, bass.ds(nn, 1)], min_val=1, max_val=E // CHUNK + 2)
                        before = sp.value_load(tiles_i[0:1, T_BEFORE2, bass.ds(nn, 1)], min_val=0, max_val=2 * TILES + 2 * E // CHUNK + 2)
                        sp.wait_ge(s["loc_done"][b], (i + L * PAIRS) * 2 + 1)
                        sp.dma_start(self_row[b][:], table[L][bass.ds(n * NT, NT), :]).then_inc(s["self_landed"][b], 16)
                        if L == 1:
                            sp.wait_ge(s["stored"][b], (i + L * PAIRS) * 16 + 16)
                            sp.dma_start(x_row[b][:], x[bass.ds(n * NT, NT), :]).then_inc(s["x2_landed"][b], 16)
                        with nc.sync.Fori(0, chunks) as c:
                            first = nc.s_assert_within(nc.sync.snap(start + c * CHUNK), 0, E, skip_runtime_bounds_check_because=
                                                       "a node tile's chunks start at one of its edges")
                            sp.wait_ge(s["gathered"][b], before + c + 1)
                            sp.wait_ge(s["dst_read"][b], before + c + 1)
                            nc.sync.sem_inc(loads_begun, 1)
                            for idx, edges in ((src_i[b], src_pad), (dst_i[b], dst_pad)):
                                sp.dma_start(idx[:, 0:IN_RUN],
                                             edges[bass.ds(first, MAIN)].rearrange("(p t) -> p t", t=IN_RUN)
                                             ).then_inc(s["idx_landed"][b], 16)
                                sp.dma_start(idx[:, IN_RUN:SLOTS],
                                             edges[bass.ds(first + MAIN, P)].rearrange("(p t) -> p t", t=1)
                                             ).then_inc(s["idx_landed"][b], 16)

        @block.gpsimd
        def _(pool):
            step = [0]

            def link(ins):
                step[0] += 1
                ins.then_inc(const_ready, 1)
                pool.wait_ge(const_ready, step[0])

            link(nc.gpsimd.memset(pad_i[:, 0, :], 0))
            link(nc.gpsimd.memset(pad_i[:, 1, :], 1 << 20))
            pool.dma_start(src_pad[E:E + PAD].rearrange("(p w) -> p w", p=P), pad_i[:, 0, :]).then_inc(rows_stored[0], 16)
            pool.dma_start(dst_pad[E:E + PAD].rearrange("(p w) -> p w", p=P), pad_i[:, 1, :]).then_inc(rows_stored[1], 16)
            for L, bias in enumerate((b0, b1)):
                pool.dma_start(b_row[0:1, L, :], bias.rearrange("(o c) -> o c", o=1)).then_inc(s["more_landed"][L], 16)
            link(nc.gpsimd.memset(a_blk[:], 0.0))
            link(nc.gpsimd.memset(ident[:], 0.0))
            link(nc.gpsimd.affine_select(out=ident[:], in_=ident[:], compare_op=ALU.not_equal, fill=1.0, base=0,
                                         pattern=[[-1, P]], channel_multiplier=1))
            link(nc.gpsimd.memset(ones[:], 1.0))
            link(nc.gpsimd.memset(eps[:], 1e-5))
            link(nc.gpsimd.iota(iota_i[:], pattern=[[1, P]], base=0, channel_multiplier=0))
            link(nc.gpsimd.iota(base_i[:], pattern=[[NT, TILES + 1]], base=0, channel_multiplier=0))
            link(nc.gpsimd.memset(reset[:], -BIG))
            for b in range(2):
                link(nc.gpsimd.memset(G[b][:, IN_RUN, :], 0.0))
            CONSTS = step[0]
            assert CONSTS == 12

            def store_group(q, i, b, sizes):
                pool.wait_ge(rows_copied[b], i * GROUP + len(sizes) + 1)
                if sizes is WHOLE:
                    pool.dma_start(group_rows(table[0], q, GROUP), row0[b][:]).then_inc(rows_stored[b], 16)
                else:
                    r = GROUPS * GROUP * P
                    pool.dma_start(table[0][r:r + P, :], row0[b][:, 0, :]).then_inc(rows_stored[b], 16)
                    pool.dma_start(table[0][r + P:N, :], row0[b][0:sizes[1], 1, :]).then_inc(rows_stored[b], 16)

            with nc.gpsimd.Fori(0, DPAIRS) as i:
                for b in range(2):
                    store_group(i * 2 + b, i, b, WHOLE)
            store_group(GROUPS, DPAIRS, 0, LAST)

            for L in range(2):
                if L == 0:
                    pool.wait_ge(tiles_ready, 1)
                    pool.wait_ge(rows_stored[0], 16 * (DPAIRS + 3))
                    pool.wait_ge(rows_stored[1], 16 * (DPAIRS + 1))
                else:
                    for b in range(2):
                        pool.wait_ge(s["stored"][b], 16 * PAIRS + 16)
                        pool.wait_ge(s["row_copied"], TILES + 1)
                with nc.gpsimd.Fori(0, PAIRS) as i:
                    for b in range(2):
                        n = i * 2 + b
                        nn = n + L * TILES
                        chunks = pool.value_load(tiles_i[0:1, T_CHUNKS, bass.ds(nn, 1)], min_val=1, max_val=E // CHUNK + 2)
                        before = pool.value_load(tiles_i[0:1, T_BEFORE2, bass.ds(nn, 1)], min_val=0, max_val=2 * TILES + 2 * E // CHUNK + 2)
                        more = pool.value_load(tiles_i[0:1, T_MORE, bass.ds(nn, 1)], min_val=0, max_val=1)
                        with nc.gpsimd.Fori(0, chunks) as c:
                            pool.wait_ge(s["summed_up"][b], before + c + 1)
                            pool.wait_ge(s["idx_landed"][b], (before + c) * 64 + 64)
                            nc.gpsimd.sem_inc(gathers_begun, 1)

                            def gather(t, landed):
                                nc.gpsimd.indirect_dma_start(
                                    out=G[b][:, t, :], out_offset=None, in_=table[L],
                                    in_offset=bass.IndirectOffsetOnAxis(ap=src_i[b][:, t:t + 1], axis=0)
                                ).then_inc(landed, 16)

                            for t in range(IN_RUN):
                                gather(t, s["lo_landed" if t < HALF else "hi_landed"][b])
                            with nc.gpsimd.If(more > 0):
                                gather(IN_RUN, s["more_landed"][b])

        @block.scalar
        def _(act):
            act.wait_ge(const_ready, 3)
            for L, (a_s, a_d) in enumerate(((a_src0, a_dst0), (a_src1, a_dst1))):
                for k, a in enumerate((a_s, a_d)):
                    for h in range(H):
                        r = h * C % P
                        act.dma_start(a_blk[r:r + C, L, h * C // P, k * H + h:k * H + h + 1],
                                      a[h:h + 1, :].rearrange("o c -> c o")).then_inc(a_landed, 16)
            act.dma_start(src_pad[0:E].rearrange("(p w) -> p w", p=EP), src.rearrange("(p w) -> p w", p=EP)).then_inc(s["stored"][0], 16)
            act.dma_start(dst_pad[0:E].rearrange("(p w) -> p w", p=EP), dst.rearrange("(p w) -> p w", p=EP)).then_inc(s["stored"][1], 16)

            def norm_group(i, b, sizes):
                m = len(sizes)
                act.wait_ge(mv_done[b], i + 1)
                nc.scalar.activation(sdev[b][:, 0:m], mv[b][:, 0:m, 1], ACT.Sqrt, bias=eps[:, 0:1]).then_inc(sdev_done[b], 1)
                act.wait_ge(shift_done[b], i + 1)
                act.wait_ge(hnT_done[0], i * 2 * GROUP // 2 + b * GROUP // 2 + 1)
                act.wait_ge(hnT_done[1], i * 2 * GROUP // 2 + b * GROUP // 2 + 1)
                for t, r in enumerate(sizes):
                    nc.scalar.activation(hn[b][0:r, t, :], xg[b][0:r, t, :], ACT.Relu,
                                         bias=shift[b][0:r, t:t + 1], scale=rstd[b][0:r, t:t + 1]).then_inc(normed[b], 1)
                act.wait_ge(rows_stored[b], i * 16 + 16)
                for t, r in enumerate(sizes):
                    act.wait_ge(rows_done[t % 2], i * GROUP + b * GROUP // 2 + t // 2 + 1 + 1)
                    nc.scalar.activation(row0[b][0:r, t, :], bank[3 + t][0:r, 0:ROW], ACT.Identity).then_inc(rows_copied[b], 1)

            with nc.scalar.Fori(0, DPAIRS) as i:
                for b in range(2):
                    norm_group(i, b, WHOLE)
            norm_group(DPAIRS, 0, LAST)

            for L in range(2):
                if L == 0:
                    act.wait_ge(tiles_ready, 1)
                else:
                    act.wait_ge(s["actT_done"], TILES + 1)
                with nc.scalar.Fori(0, PAIRS) as i:
                    for b in range(2):
                        n = i * 2 + b
                        nn = n + L * TILES
                        chunks = act.value_load(tiles_i[0:1, T_CHUNKS, bass.ds(nn, 1)], min_val=1, max_val=E // CHUNK + 2)
                        before = act.value_load(tiles_i[0:1, T_BEFORE, bass.ds(nn, 1)], min_val=0, max_val=2 * TILES + 2 * E // CHUNK + 2)
                        before2 = act.value_load(tiles_i[0:1, T_BEFORE2, bass.ds(nn, 1)], min_val=0, max_val=2 * TILES + 2 * E // CHUNK + 2)
                        used = act.value_load(tiles_i[0:1, T_MORE2, bass.ds(nn, 1)], min_val=0, max_val=2 * TILES + 2 * E // CHUNK + 2)
                        more = act.value_load(tiles_i[0:1, T_MORE, bass.ds(nn, 1)], min_val=0, max_val=1)
                        act.wait_ge(s["self_landed"][b], (i + L * PAIRS) * 16 + 16)
                        act.wait_ge(s["mean_ready"], nn + 1)
                        nc.scalar.activation(state[:, 0:HC], self_row[b][:, 0:HC], ACT.Identity).then_inc(s["loc_done"][b], 1)
                        with nc.scalar.Fori(0, chunks) as c:
                            g = nc.scalar.snap(before + c)
                            g1 = nc.scalar.snap(before + c + 1)
                            p1 = nc.scalar.snap(before2 + c + 1)
                            act.wait_ge(s["edge_done"], g + 1)
                            for r in range(0, SLOTS, 4):
                                m = min(4, SLOTS - r)
                                k = r // 4
                                act.wait_ge(s["onehotT_done"][k % 2], g * (3 - k % 2) + k // 2 + 1)
                                nc.scalar.activation(onehotT[:, r:r + m, :],
                                                     bank[3 + k % 2][0:NT, 0:m * P].rearrange("d (t e) -> d t e", e=P),
                                                     ACT.Identity).then_inc(s["onehotT_copied"][k % 2], 1)
                            act.wait_ge(s["away_ready"], g1)
                            act.wait_ge(s["max_ready"], g1)
                            act.wait_ge(s["spreadT_done"], g + 1)
                            for j in range(2):
                                if j == 1:
                                    act.wait_ge(s["more_landed"][b], (used + c + more) * 16 + 16)
                                for h in range(H):
                                    value = run_max[:, h, IN_RUN - 1:IN_RUN] if j == 0 else G[b][:, IN_RUN, HC + h:HC + h + 1]
                                    last = nc.scalar.activation(spread[:, j, h, :], away[:, j, :], ACT.Identity, bias=value)
                            last.then_inc(s["spread_ready"], 1)
                            act.wait_ge(s["fall_ready"], g1)
                            nc.scalar.activation(scale[:], fall[:], ACT.Exp).then_inc(s["scale_ready"], 1)
                            act.wait_ge(s["c_ready"], g1)
                            nc.scalar.activation(G[b][:, :, HC:HC + H], ce[:], ACT.Exp).then_inc(s["w_ready"], 1)
                            act.wait_ge(s["summed_up"][b], p1 + 1)
                            nc.scalar.activation(state[:], bank[5][0:NT, 0:HC + H], ACT.Identity).then_inc(s["state_moved"], 1)
                        act.wait_ge(s["o_ready"], nn + 1)
                        if L == 0:
                            act.wait_ge(s["actT_done"], n + 1)
                        else:
                            act.wait_ge(s["y_ready_out"], n + 1)
                        nc.scalar.activation(act_o[:], o[:], ACT.Gelu).then_inc(s["act_ready"], 1)
                        if L == 0:
                            act.wait_ge(s["row_done"], n + 1)
                            act.wait_ge(s["actT_done"], n + 1 + 1)
                            nc.scalar.activation(act_oT[:], bank[6][:, 0:KC * NT].rearrange("c (k n) -> c k n", n=NT),
                                                 ACT.Identity).then_inc(s["actT_copied"], 1)
                            act.wait_ge(s["row_done"], n + 1 + 1)
                            act.wait_ge(s["stored"][1 - b], (i + b + L * PAIRS) * 16 + 16)
                            nc.scalar.activation(row1[:], bank[7][0:NT, 0:ROW], ACT.Identity).then_inc(s["row_copied"], 1)
                            act.wait_ge(s["row_copied"], n + 1 + 1)
                            act.dma_start(table[1][bass.ds(n * NT, NT), :], row1[:]).then_inc(s["stored"][b], 16)
                        else:
                            act.wait_ge(s["y_ready_out"], n + 1 + 1)
                            act.dma_start(out[bass.ds(n * NT, NT), :], y_out[:]).then_inc(s["stored"][b], 16)
            for b in range(2):
                act.wait_ge(s["stored"][b], 16 * 2 * PAIRS + 16)

        @block.vector
        def _(dve):
            step = [0]

            def link(ins):
                step[0] += 1
                ins.then_inc(prep_step, 1)
                dve.wait_ge(prep_step, step[0])

            dve.wait_ge(const_ready, 12)
            nc.vector.tensor_copy(iota_f[:], iota_i[:])
            link(nc.vector.tensor_copy(base_f[:], base_i[:]))
            for L in range(2):
                dve.wait_ge(wT_done, L + 1)
                nc.vector.tensor_copy(w_t[:, L], bank[1 + L][:, :].rearrange("p (k c) -> p k c", k=KC)).then_inc(wT_copied, 1)
            dve.wait_ge(w_landed, 32)
            for L in range(2):
                nc.vector.tensor_copy(w_ext[:, L, :, 0:D], w_in[:, L])
            dve.wait_ge(wa_done, 1)
            nc.vector.tensor_copy(w_ext[:, :, :, D:ROW],
                                  bank[0][:, 0:2 * KC * 2 * H].rearrange("p (l k a) -> p l k a", l=2, k=KC)).then_inc(w_ext_ready, 1)
            dve.wait_ge(b_done, 1)
            nc.vector.tensor_copy(b_all[:], bank[7][:, :].rearrange("p (l c) -> p l c", l=2))

            dve.wait_ge(dst_landed, 16)
            link(nc.vector.tensor_copy(samp[:], dst_all[:].rearrange("p (a s) -> p a s", s=STRIDE)[:, :, 0]))
            link(nc.vector.tensor_tensor(below[:], wide(samp[:], 1, TILES + 1), wide(base_f[0:EP, :], 2, SAMPLES), ALU.is_lt))
            nc.vector.tensor_reduce(count[:], below[:], AX.X, ALU.add).then_inc(count_ready, 1)

            def stats_group(i, b, sizes):
                dve.wait_ge(x_landed[b], i * 16 + 16 * (1 if sizes is WHOLE else 2))
                for t, r in enumerate(sizes):
                    last = nc.vector.bn_stats(stats[b][0:r, t, :], xg[b][0:r, t, :])
                last.then_inc(stats_done[b], 1)
                dve.wait_ge(stats_done[b], i + 1)
                nc.vector.sem_inc(aggr_begun, 1)
                for t, r in enumerate(sizes):
                    last = nc.vector.bn_aggr(mv[b][0:r, t, :], stats[b][0:r, t, :])
                last.then_inc(mv_done[b], 1)
                dve.wait_ge(sdev_done[b], i + 1)
                m = len(sizes)
                nc.vector.reciprocal(rstd[b][:, 0:m], sdev[b][:, 0:m]).then_inc(rstd_done[b], 1)
                dve.wait_ge(rstd_done[b], i + 1)
                nc.vector.scalar_tensor_tensor(out=shift[b][:, 0:m], in0=mv[b][:, 0:m, 0], scalar=-1.0,
                                               in1=rstd[b][:, 0:m], op0=ALU.mult, op1=ALU.mult).then_inc(shift_done[b], 1)

            def copy_group(i, b, sizes):
                for t, r in enumerate(sizes):
                    k = t % 2
                    turn = i * GROUP + b * GROUP // 2 + t // 2
                    dve.wait_ge(rows_done[k], turn + 1)
                    dve.wait_ge(hnT_done[k], turn + 1 + 1)
                    nc.vector.tensor_copy(hnT[k][:, :, 0:r], bank[1 + k][:, 0:KC * P].rearrange("c (k n) -> c k n", n=P)[:, :, 0:r]
                                          ).then_inc(hnT_copied[k], 1)

            with nc.vector.Fori(0, DPAIRS) as i:
                for b in range(2):
                    stats_group(i, b, WHOLE)
                    copy_group(i, b, WHOLE)
            stats_group(DPAIRS, 0, LAST)
            copy_group(DPAIRS, 0, LAST)

            dve.wait_ge(rank_done, 1)
            link(nc.vector.tensor_copy(rank[:], bank[0][:, 256:256 + TILES + 1]))
            link(nc.vector.tensor_scalar(start_f[:], rank[:, 0:TILES], -1.0, float(STRIDE), ALU.add, ALU.mult))
            link(nc.vector.tensor_scalar(start_f[:], start_f[:], 0.0, None, ALU.max))
            link(nc.vector.tensor_scalar(last_f[:], rank[:, 1:TILES + 1], float(STRIDE), -1.0, ALU.mult, ALU.add))
            link(nc.vector.tensor_tensor(last_f[:], last_f[:], start_f[:], ALU.subtract))
            link(nc.vector.tensor_scalar(last_f[:], last_f[:], 0.0, None, ALU.max))
            link(nc.vector.tensor_copy(last_i[:], last_f[:]))
            link(nc.vector.tensor_scalar(full_i[:], last_i[:], 7, None, ALU.arith_shift_right))
            link(nc.vector.tensor_copy(full_f[:], full_i[:]))
            link(nc.vector.tensor_scalar(more_f[:], full_f[:], float(IN_RUN), None, ALU.is_ge))
            link(nc.vector.tensor_scalar(last_f[:], full_f[:], float(65536 // SLOTS + 1), None, ALU.mult))
            link(nc.vector.tensor_copy(last_i[:], last_f[:]))
            link(nc.vector.tensor_scalar(full_i[:], last_i[:], 16, None, ALU.arith_shift_right))
            link(nc.vector.tensor_copy(chunks_f[:], wide(full_i[:], 1, 2)))
            link(nc.vector.tensor_scalar(chunks_f[:], chunks_f[:], 1.0, None, ALU.add))
            all_chunks = chunks_f[:].rearrange("p l n -> p (l n)")
            link(nc.vector.tensor_tensor_scan(cum_f[:], all_chunks, all_chunks, 0.0, ALU.add, ALU.bypass))
            link(nc.vector.tensor_tensor(cum_f[:], cum_f[:], all_chunks, ALU.subtract))
            link(nc.vector.tensor_tensor(used_f[:], chunks_f[:], wide(more_f[:], 1, 2), ALU.mult))
            all_used = used_f[:].rearrange("p l n -> p (l n)")
            for b in range(2):
                for counted, row in ((all_chunks, T_BEFORE2), (all_used, T_MORE2)):
                    link(nc.vector.tensor_tensor_scan(cump_f[:, b, :], counted[:, b::2], counted[:, b::2], 0.0, ALU.add, ALU.bypass))
                    link(nc.vector.tensor_tensor(cump_f[:, b, :], cump_f[:, b, :], counted[:, b::2], ALU.subtract))
                    link(nc.vector.tensor_copy(tiles_i[:, row, b::2], cump_f[:, b, :]))
            link(nc.vector.tensor_copy(tiles_i[:, T_START, :].rearrange("p (l n) -> p l n", l=2), wide(start_f[:], 1, 2)))
            link(nc.vector.tensor_copy(tiles_i[:, T_CHUNKS, :], all_chunks))
            link(nc.vector.tensor_copy(tiles_i[:, T_MORE, :].rearrange("p (l n) -> p l n", l=2), wide(more_f[:], 1, 2)))
            link(nc.vector.tensor_copy(tiles_i[:, T_BEFORE, :], cum_f[:]))
            nc.vector.tensor_copy(rank[:, 0:1], start_f[:, 0:1]).then_inc(tiles_ready, 1)

            for L in range(2):
                with nc.vector.Fori(0, PAIRS) as i:
                    for b in range(2):
                        n = i * 2 + b
                        nn = n + L * TILES
                        chunks = dve.value_load(tiles_i[0:1, T_CHUNKS, bass.ds(nn, 1)], min_val=1, max_val=E // CHUNK + 2)
                        before = dve.value_load(tiles_i[0:1, T_BEFORE, bass.ds(nn, 1)], min_val=0, max_val=2 * TILES + 2 * E // CHUNK + 2)
                        before2 = dve.value_load(tiles_i[0:1, T_BEFORE2, bass.ds(nn, 1)], min_val=0, max_val=2 * TILES + 2 * E // CHUNK + 2)
                        used = dve.value_load(tiles_i[0:1, T_MORE2, bass.ds(nn, 1)], min_val=0, max_val=2 * TILES + 2 * E // CHUNK + 2)
                        more = dve.value_load(tiles_i[0:1, T_MORE, bass.ds(nn, 1)], min_val=0, max_val=1)
                        dve.wait_ge(s["self_landed"][b], (i + L * PAIRS) * 16 + 16)
                        nc.vector.memset(state[:, HC:HC + H], 1.0)
                        nc.vector.tensor_copy(cands[:, :, 3], self_row[b][:, HC:HC + H])
                        nc.vector.tensor_copy(maxes[:, 0, :], self_row[b][:, HC:HC + H]).then_inc(s["misc_set"], 1)
                        nc.vector.tensor_copy(logit[:, 2, :], self_row[b][:, HC + H:ROW]).then_inc(s["loc_done"][b], 1)
                        with nc.vector.Fori(0, chunks) as c:
                            g = nc.vector.snap(before + c)
                            g1 = nc.vector.snap(before + c + 1)
                            p1 = nc.vector.snap(before2 + c + 1)
                            dve.wait_ge(s["idx_landed"][b], p1 * 64)
                            nc.vector.tensor_scalar(dloc[:], dst_i[b][:], base_f[:, bass.ds(n, 1)], None, ALU.subtract
                                                    ).then_inc(s["dst_read"][b], 1)
                            dve.wait_ge(s["state_moved"], g + 1)
                            dve.wait_ge(s["dst_read"][b], p1 + 1)
                            nc.vector.tensor_tensor(onehot[:], wide(iota_f[:, 0:NT], 1, SLOTS), wide(dloc[:], 2, NT), ALU.is_equal
                                                    ).then_inc(s["onehot_ready"], 1)
                            nc.vector.tensor_tensor(ends[:], dloc[:, 0:IN_RUN - 1], dloc[:, 1:IN_RUN], ALU.not_equal
                                                    ).then_inc(s["ends_ready"], 1)
                            dve.wait_ge(s["ends_ready"], g1)
                            nc.vector.tensor_scalar(reset[:, :, 1:IN_RUN], wide(ends[:], 1, H), -BIG, None, ALU.mult)
                            dve.wait_ge(s["onehot_ready"], g1)
                            nc.vector.tensor_scalar(away[:], onehot[:, IN_RUN - 1:SLOTS, :], -1.0, BIG, ALU.add, ALU.mult
                                                    ).then_inc(s["away_ready"], 1)
                            dve.wait_ge(s["lo_landed"][b], p1 * (16 * HALF))
                            dve.wait_ge(s["hi_landed"][b], p1 * (16 * HALF))
                            nc.vector.tensor_copy(a_run[:], G[b][:, 0:IN_RUN, HC:HC + H].rearrange("p t h -> p h t")
                                                  ).then_inc(s["run_ready"], 1)
                            dve.wait_ge(s["run_ready"], g1)
                            dve.wait_ge(s["away_ready"], g1)
                            nc.vector.tensor_tensor_scan(run_max[:].rearrange("p h t -> p (h t)"),
                                                         reset[:].rearrange("p h t -> p (h t)"),
                                                         a_run[:].rearrange("p h t -> p (h t)"), 0.0, ALU.add, ALU.max
                                                         ).then_inc(s["max_ready"], 1)
                            dve.wait_ge(s["max_ready"], g1)
                            nc.vector.tensor_copy(marked[:, :, H], ends[:])
                            nc.vector.tensor_tensor(marked[:, :, 0:H], run_max[:, :, 0:IN_RUN - 1].rearrange("p h t -> p t h"),
                                                    wide(ends[:], 2, H), ALU.mult).then_inc(s["marked_ready"], 1)
                            dve.wait_ge(s["runs_done"], g1)
                            runs = bank[0][0:NT, 0:(IN_RUN - 1) * (H + 1)].rearrange("d (t a) -> d t a", a=H + 1)
                            nc.vector.tensor_scalar(absent[:], runs[:, :, H], -1.0, BIG, ALU.add, ALU.mult).then_inc(s["absent_ready"], 1)
                            dve.wait_ge(s["absent_ready"], g1)
                            nc.vector.tensor_tensor(seg[:], runs[:, :, 0:H].rearrange("d t h -> d h t"), wide(absent[:], 1, H), ALU.add
                                                    ).then_inc(s["seg_ready"], 1)
                            dve.wait_ge(s["seg_ready"], g1)
                            nc.vector.tensor_reduce(cands[:, :, 0], seg[:], AX.X, ALU.max)
                            dve.wait_ge(s["spreadT_done"], g1 + 1)
                            for j in range(2):
                                last = nc.vector.tensor_reduce(cands[:, :, 1 + j], bank[1 + j][0:NT, :].rearrange("d (h e) -> d h e", e=P),
                                                               AX.X, ALU.max)
                            last.then_inc(s["cands_ready"], 1)
                            dve.wait_ge(s["cands_ready"], g1)
                            nc.vector.tensor_reduce(maxes[:, 1, :], cands[:], AX.X, ALU.max).then_inc(s["newmax_done"], 1)
                            dve.wait_ge(s["newmax_done"], g1)
                            nc.vector.tensor_tensor(summed[:], maxes[:], wide(logit[:, 2, :], 1, 2), ALU.add).then_inc(s["sum_ready"], 1)
                            dve.wait_ge(s["sum_ready"], g1)
                            nc.vector.scalar_tensor_tensor(out=logit[:, 0:2, :], in0=summed[:], scalar=0.2, in1=summed[:],
                                                           op0=ALU.mult, op1=ALU.max).then_inc(s["logit_ready"], 1)
                            nc.vector.tensor_copy(cands[:, :, 3], maxes[:, 1, :])
                            nc.vector.tensor_copy(maxes[:, 0, :], maxes[:, 1, :])
                            dve.wait_ge(s["logit_ready"], g1)
                            nc.vector.tensor_tensor(fall[:], logit[:, 0, :], logit[:, 1, :], ALU.subtract).then_inc(s["fall_ready"], 1)
                            edge = bank[0][:, 128:128 + SLOTS * 2 * H].rearrange("p (t k h) -> p t k h", k=2, h=H)
                            dve.wait_ge(s["edge_done"], g1 + 1)
                            dve.wait_ge(s["more_landed"][b], (used + c + more) * 16 + 16)
                            nc.vector.tensor_tensor(ye[:], G[b][:, :, HC:HC + H], edge[:, :, 1, :], ALU.add).then_inc(s["gathered"][b], 1)
                            dve.wait_ge(s["gathered"][b], p1 + 1)
                            nc.vector.scalar_tensor_tensor(out=ze[:], in0=ye[:], scalar=0.2, in1=ye[:], op0=ALU.mult, op1=ALU.max
                                                           ).then_inc(s["z_ready"], 1)
                            dve.wait_ge(s["z_ready"], g1)
                            nc.vector.tensor_tensor(de[:], ze[:], edge[:, :, 0, :], ALU.subtract).then_inc(s["d_ready"], 1)
                            dve.wait_ge(s["d_ready"], g1)
                            nc.vector.tensor_scalar(ce[:], de[:], 0.0, None, ALU.min).then_inc(s["c_ready"], 1)
                            dve.wait_ge(s["scale_ready"], g1)
                            dve.wait_ge(s["loc_done"][b], (i + L * PAIRS) * 2 + 2 + 1)
                            dve.wait_ge(s["misc_set"], nn + 1)
                            nc.vector.tensor_tensor(scaled[:, 0:HC].rearrange("d (h c) -> d h c", h=H),
                                                    state[:, 0:HC].rearrange("d (h c) -> d h c", h=H), wide(scale[:], 2, C), ALU.mult)
                            nc.vector.tensor_tensor(scaled[:, HC:HC + H], state[:, HC:HC + H], scale[:], ALU.mult).then_inc(s["scaled_ready"], 1)
                            dve.wait_ge(s["w_ready"], g1)
                            for t0, t1 in ((0, 6), (6, 12), (12, SLOTS)):
                                rows = G[b][:, t0:t1, 0:HC].rearrange("p t (h c) -> p t h c", h=H)
                                nc.vector.tensor_tensor(rows, rows, wide(G[b][:, t0:t1, HC:HC + H], 3, C), ALU.mult
                                                        ).then_inc(s["part_weighted"][t0 // 6], 1)
                        dve.wait_ge(s["state_moved"], before + chunks + 1)
                        nc.vector.reciprocal(inv[:], state[:, HC:HC + H]).then_inc(s["inv_ready"], 1)
                        dve.wait_ge(s["inv_ready"], nn + 1)
                        nc.vector.tensor_tensor(mean_o[:].rearrange("d (h c) -> d h c", h=H),
                                                state[:, 0:HC].rearrange("d (h c) -> d h c", h=H), wide(inv[:], 2, C), ALU.mult
                                                ).then_inc(s["mean_ready"], 1)
                        dve.wait_ge(s["mean_ready"], nn + 1 + 1)
                        dve.wait_ge(s["act_ready"], nn + 1)
                        nc.vector.tensor_tensor(o[:], mean_o[:], b_all[0:NT, L, :], ALU.add).then_inc(s["o_ready"], 1)
                        if L == 1:
                            dve.wait_ge(s["x2_landed"][b], i * 16 + 16)
                            dve.wait_ge(s["act_ready"], nn + 1 + 1)
                            dve.wait_ge(s["stored"][1 - b], (i + b + L * PAIRS) * 16 + 16)
                            nc.vector.tensor_tensor(y_out[:], act_o[:], x_row[b][:], ALU.add).then_inc(s["y_ready_out"], 1)

        @block.tensor
        def _(pe):
            pe.wait_ge(const_ready, 12)
            pe.wait_ge(w_landed, 32)
            for L in range(2):
                for k in range(KC):
                    for j in range(KC):
                        last = nc.tensor.transpose(bank[1 + L][:, k * D + j * P:k * D + (j + 1) * P],
                                                   w_in[:, L, j, k * P:(k + 1) * P], ident[:])
                last.then_inc(wT_done, 1)
            for L in range(2):
                pe.wait_ge(s["more_landed"][L], 16)
            nc.tensor.matmul(bank[7][:, :], ones[0:1, :], b_row[0:1, :, :].rearrange("o l c -> o (l c)"),
                             start=True, stop=True).then_inc(b_done, 1)
            pe.wait_ge(a_landed, 16 * 4 * H)
            pe.wait_ge(wT_copied, 2)
            for L in range(2):
                for j in range(KC):
                    for k in range(KC):
                        o0 = (L * KC + j) * 2 * H
                        last = nc.tensor.matmul(bank[0][:, o0:o0 + 2 * H], w_t[:, L, k, j * P:(j + 1) * P],
                                                a_blk[:, L, k, :], start=(k == 0), stop=(k == KC - 1))
            last.then_inc(wa_done, 1)
            pe.wait_ge(count_ready, 1)
            nc.tensor.matmul(bank[0][:, 256:256 + TILES + 1], ones[0:EP, :], count[:], start=True, stop=True).then_inc(rank_done, 1)
            pe.wait_ge(w_ext_ready, 1)

            def dense_group(i, b, sizes):
                for t, r in enumerate(sizes):
                    k = t % 2
                    turn = i * GROUP + b * GROUP // 2 + t // 2
                    pe.wait_ge(hnT_copied[k], turn + 1)
                    pe.wait_ge(normed[b], i * GROUP + t + 1 + 1)
                    for j in range(KC):
                        last = nc.tensor.transpose(bank[1 + k][:, j * P:j * P + r], hn[b][0:r, t, j * P:(j + 1) * P], ident[0:r, 0:r])
                    last.then_inc(hnT_done[k], 1)
                    pe.wait_ge(rows_copied[1 - b], (i + b) * GROUP + 1)
                    pe.wait_ge(hnT_copied[k], turn + 1 + 1)
                    for j in range(KC):
                        last = nc.tensor.matmul(bank[3 + t][0:r, 0:ROW], hnT[k][:, j, 0:r], w_ext[:, 0, j, :],
                                                start=(j == 0), stop=(j == KC - 1))
                    last.then_inc(rows_done[k], 1)

            with nc.tensor.Fori(0, DPAIRS) as i:
                for b in range(2):
                    dense_group(i, b, WHOLE)
            dense_group(DPAIRS, 0, LAST)

            for L in range(2):
                if L == 0:
                    pe.wait_ge(tiles_ready, 1)
                    pe.wait_ge(rows_copied[0], DPAIRS * GROUP + len(LAST) + 1)
                    pe.wait_ge(rows_copied[1], DPAIRS * GROUP + 1)
                with nc.tensor.Fori(0, PAIRS) as i:
                    for b in range(2):
                        n = i * 2 + b
                        nn = n + L * TILES
                        chunks = pe.value_load(tiles_i[0:1, T_CHUNKS, bass.ds(nn, 1)], min_val=1, max_val=E // CHUNK + 2)
                        before = pe.value_load(tiles_i[0:1, T_BEFORE, bass.ds(nn, 1)], min_val=0, max_val=2 * TILES + 2 * E // CHUNK + 2)
                        with nc.tensor.Fori(0, chunks) as c:
                            g = nc.tensor.snap(before + c)
                            g1 = nc.tensor.snap(before + c + 1)
                            pe.wait_ge(s["onehot_ready"], g1)
                            for r in range(0, SLOTS, 4):
                                m = min(4, SLOTS - r)
                                k = r // 4
                                pe.wait_ge(s["onehotT_copied"][k % 2], g * (3 - k % 2) + k // 2 + 1)
                                for t in range(r, r + m):
                                    last = nc.tensor.transpose(bank[3 + k % 2][0:NT, (t - r) * P:(t - r + 1) * P], onehot[:, t, :], ident[:])
                                last.then_inc(s["onehotT_done"][k % 2], 1)
                            pe.wait_ge(s["marked_ready"], g1)
                            for t in range(IN_RUN - 1):
                                last = nc.tensor.matmul(bank[0][0:NT, t * (H + 1):(t + 1) * (H + 1)], onehot[:, t, :], marked[:, t, :],
                                                        start=True, stop=True)
                            last.then_inc(s["runs_done"], 1)
                            pe.wait_ge(s["spread_ready"], g1)
                            for j in range(2):
                                for h in range(H):
                                    last = nc.tensor.transpose(bank[1 + j][0:NT, h * P:(h + 1) * P], spread[:, j, h, :], ident[:])
                            last.then_inc(s["spreadT_done"], 1)
                            pe.wait_ge(s["onehotT_copied"][0], g * 3 + 3 + 1)
                            pe.wait_ge(s["onehotT_copied"][1], g * 2 + 2 + 1)
                            pe.wait_ge(s["logit_ready"], g1)
                            for t in range(SLOTS):
                                last = nc.tensor.matmul(bank[0][:, 128 + t * 2 * H:128 + (t + 1) * 2 * H], onehotT[:, t, :],
                                                        logit[:, 1:3, :].rearrange("d k h -> d (k h)"), start=True, stop=True)
                            last.then_inc(s["edge_done"], 1)
                            pe.wait_ge(s["scaled_ready"], g1)
                            nc.tensor.matmul(bank[5][0:NT, 0:HC + H], ident[0:NT, 0:NT], scaled[:], start=True, stop=False)
                            for t in range(SLOTS):
                                if t % 6 == 0 and t < 18:
                                    pe.wait_ge(s["part_weighted"][t // 6], g1)
                                last = nc.tensor.matmul(bank[5][0:NT, 0:HC + H], onehot[:, t, :], G[b][:, t, 0:HC + H],
                                                        start=False, stop=(t == SLOTS - 1))
                            last.then_inc(s["summed_up"][b], 1)
                        if L == 0:
                            pe.wait_ge(s["act_ready"], nn + 1 + 1)
                            for k in range(KC):
                                last = nc.tensor.transpose(bank[6][:, k * NT:(k + 1) * NT], act_o[:, k * P:(k + 1) * P], ident[0:NT, 0:NT])
                            last.then_inc(s["actT_done"], 1)
                            pe.wait_ge(s["row_copied"], n + 1)
                            pe.wait_ge(s["actT_copied"], n + 1)
                            for k in range(KC):
                                last = nc.tensor.matmul(bank[7][0:NT, 0:ROW], act_oT[:, k, :], w_ext[:, 1, k, :],
                                                        start=(k == 0), stop=(k == KC - 1))
                            last.then_inc(s["row_done"], 1)


_INS = ["x", "src", "dst", "edge_attr_32", "L0_gnn_W0", "L0_gnn_a_src0", "L0_gnn_a_dst0", "L0_gnn_b0",
        "L0_gnn_W1", "L0_gnn_a_src1", "L0_gnn_a_dst1", "L0_gnn_b1"]
_OUTS = [((12500, 256), "float32")]


def kernel(**inputs):
    import numpy as _np
    import concourse.bacc as _bacc
    from concourse import mybir as _mybir
    from concourse.bass_utils import run_bass_kernel_spmd as _run

    nc = _bacc.Bacc("TRN2", target_bir_lowering=False, num_devices=1)
    arrays, args = {}, []
    for name in _INS:
        a = _np.ascontiguousarray(inputs[name])
        arrays[f"in_{name}_dram"] = a
        args.append(nc.dram_tensor(f"in_{name}_dram", a.shape, _mybir.dt.from_np(a.dtype), kind="ExternalInput").ap())
    for i, (shape, dtype) in enumerate(_OUTS):
        dt = _mybir.dt.from_np(_np.dtype(dtype))
        args.append(nc.dram_tensor(f"out_{i}_dram", shape, dt, kind="ExternalOutput").ap())
    two_layer_graph_attention(nc, *args)
    r = _run(nc, [arrays], core_ids=[0])
    got = tuple(r.results[0][f"out_{i}_dram"] for i in range(len(_OUTS)))
    return got[0]
```

```python
from contextlib import ExitStack

import concourse.bass as bass
from concourse import mybir

ALU = mybir.AluOpType
ACT = mybir.ActivationFunctionType
AX = mybir.AxisListType
F32 = mybir.dt.float32
BF16 = mybir.dt.bfloat16
I32 = mybir.dt.int32

P = 128
BIG = 1.0e30


def wide(ap, axis, n):
    shape = list(ap.shape)
    return ap.unsqueeze(axis).broadcast_to(shape[:axis] + [n] + shape[axis:])


def two_layer_graph_attention(nc, x, src, dst, edge_attr, W0, a_src0, a_dst0, b0, W1, a_src1, a_dst1, b1, out):
    N, D = x.shape
    E = src.shape[0]
    H, C = a_src0.shape
    HC = H * C
    ROW = HC + 2 * H
    KC = D // P

    NT = 125
    TILES = N // NT
    PAIRS = TILES // 2
    IN_RUN = E // TILES // P + 1
    SLOTS = IN_RUN + 1
    CHUNK = SLOTS * P
    MAIN = IN_RUN * P
    HALF = IN_RUN // 2
    STRIDE = 16
    EP = 125
    EW = E // EP
    SAMPLES = EW // STRIDE
    PAD = CHUNK + P
    NB = 4
    STEPS = -(-(TILES + (E + TILES * 2 * STRIDE) // CHUNK) // NB) * NB
    HALF_STEPS = STEPS // 2
    PARTS = [(0, 5), (5, 10), (10, 14), (14, SLOTS)]
    assert TILES % NB == 0 and E % (EP * STRIDE) == 0 and D == HC and KC == 2 and IN_RUN == 16

    GROUP = 4
    GROUPS = N // (GROUP * P)
    REST = N - GROUPS * GROUP * P
    DPAIRS = GROUPS // 2
    assert GROUPS % 2 == 0 and P < REST <= 2 * P

    with ExitStack() as ctx:
        def sb(name, shape, dt=F32):
            return ctx.enter_context(nc.sbuf_tensor(name, shape, dt))

        def sem(name):
            return ctx.enter_context(nc.semaphore(name))

        def dram(name, shape, dt):
            return nc.dram_tensor(name, shape, dt, kind="Internal").ap()

        table = [dram("table0", [N, ROW], F32), dram("table1", [N, ROW], F32)]
        src_pad = dram("src_pad", [E + PAD], I32)
        dst_pad = dram("dst_pad", [E + PAD], I32)

        bank = [ctx.enter_context(nc.psum_tensor(f"bank{i}", [P, 512], F32)) for i in range(8)]

        rows_all = sb("rows_all", [P, NB, SLOTS, ROW])
        G = [rows_all[:, u] for u in range(NB)]
        spare = rows_all[0:EP].rearrange("p u t c -> p (u t c)")
        dst_all = spare[:, 0:EW].bitcast(I32)
        below = spare[:, EW:EW + -(-(TILES + 1) * SAMPLES // 2)].bitcast(BF16).rearrange("p (n a) -> p n a", a=SAMPLES)

        ident = sb("ident", [P, P])
        ones = sb("ones", [P, P])
        iota_i = sb("iota_i", [P, P], I32)
        iota_f = sb("iota_f", [P, P])
        iota_b = sb("iota_b", [P, P], BF16)
        ident_b = sb("ident_b", [P, P], BF16)
        base_i = sb("base_i", [P, TILES + 1], I32)
        base_f = sb("base_f", [P, TILES + 1])
        eps = sb("eps", [P, 1])
        w_in = sb("w_in", [P, 2, KC, D])
        w_t = sb("w_t", [P, 2, KC, D])
        a_blk = sb("a_blk", [P, 2, KC, 2 * H])
        w_ext = sb("w_ext", [P, 2, KC, ROW])
        b_row = sb("b_row", [1, 2, HC])
        b_all = sb("b_all", [P, 2, HC])
        pad_i = sb("pad_i", [P, 2, PAD // P], I32)

        samp = sb("samp", [EP, SAMPLES])
        count = sb("count", [EP, TILES + 1])
        rank = sb("rank", [P, TILES + 1])
        first_edge = sb("first_edge", [P, TILES])
        span = sb("span", [P, TILES])
        span_i = sb("span_i", [P, TILES], I32)
        full = sb("full", [P, TILES])
        more = sb("more", [P, TILES])
        chunks = sb("chunks", [P, TILES])
        upto = sb("upto", [P, TILES])
        prior = sb("prior", [P, TILES])
        step_no = sb("step_no", [P, 2])
        step_no_i = sb("step_no_i", [P, 2], I32)
        pick = sb("pick", [HALF_STEPS, 2, TILES])
        picked = sb("picked", [HALF_STEPS, 2, TILES])
        tile_of = sb("tile_of", [HALF_STEPS, 2])
        inside = sb("inside", [HALF_STEPS, 2])
        nth = sb("nth", [HALF_STEPS, 2])
        F_TILE, F_BASE, F_EDGE, F_MORE, F_FIRST, F_LATER = range(6)
        field = sb("field", [HALF_STEPS, 6, 2])
        steps = sb("steps", [P, 6, 2 * STEPS])
        T_TILE, T_EDGE, T_MORE, T_USED = range(4)
        steps_i = sb("steps_i", [P, 4, 2 * STEPS], I32)
        quads_f = sb("quads_f", [P, 1])
        quads_i = sb("quads_i", [P, 1], I32)
        rounds = sb("rounds", [P, 1], I32)
        used = sb("used", [P, 2 * STEPS // NB])

        xg = [sb(f"xg{b}", [P, GROUP, D]) for b in range(2)]
        hn = [sb(f"hn{b}", [P, GROUP, D]) for b in range(2)]
        stats = [sb(f"stats{b}", [P, GROUP, 6]) for b in range(2)]
        mv = [sb(f"mv{b}", [P, GROUP, 2]) for b in range(2)]
        sdev = [sb(f"sdev{b}", [P, GROUP]) for b in range(2)]
        rstd = [sb(f"rstd{b}", [P, GROUP]) for b in range(2)]
        shift = [sb(f"shift{b}", [P, GROUP]) for b in range(2)]
        hnT = [sb(f"hnT{b}", [P, KC, P]) for b in range(2)]
        row0 = [sb(f"row0{b}", [P, GROUP, ROW]) for b in range(2)]

        src_i = [sb(f"src_i{u}", [P, SLOTS], I32) for u in range(NB)]
        dst_i = [sb(f"dst_i{u}", [P, SLOTS], I32) for u in range(NB)]
        self_row = [sb(f"self_row{u}", [NT, ROW]) for u in range(NB)]
        x_row = [sb(f"x_row{u}", [NT, D]) for u in range(NB)]
        dloc = sb("dloc", [P, SLOTS], BF16)
        onehot = sb("onehot", [P, SLOTS, NT], BF16)
        onehot_f = [sb(f"onehot_f{k}", [P, SLOTS, NT]) for k in range(2)]
        onehotT = sb("onehotT", [NT, SLOTS, P], BF16)
        ends = sb("ends", [P, IN_RUN - 1])
        reset = sb("reset", [P, H, IN_RUN])
        away = sb("away", [P, 2, NT])
        a_run = sb("a_run", [P, H, IN_RUN])
        run_max = sb("run_max", [P, H, IN_RUN])
        at_end = sb("at_end", [P, IN_RUN - 1, H])
        at_end_r = sb("at_end_r", [P, IN_RUN - 1, H])
        marked = sb("marked", [P, IN_RUN - 1, 3 * H + 1], BF16)
        spread = sb("spread", [P, 2, H, NT])
        absent = sb("absent", [NT, IN_RUN - 1])
        seg_sum = sb("seg_sum", [NT, H, IN_RUN - 1])
        seg = sb("seg", [NT, H, IN_RUN - 1])
        cands = sb("cands", [NT, H, 4])
        own = sb("own", [NT, H])
        maxes = sb("maxes", [NT, 2, H])
        summed = sb("summed", [NT, 2, H])
        logit = sb("logit", [NT, 3, H])
        logit_r = sb("logit_r", [NT, 2, H])
        logit_p = sb("logit_p", [NT, 3, 2, H], BF16)
        fall = sb("fall", [NT, H])
        scale = [sb(f"scale{k}", [NT, H]) for k in range(2)]
        begin = [sb(f"begin{k}", [NT, HC + H]) for k in range(2)]
        state = sb("state", [NT, HC + H])
        chosen = sb("chosen", [NT, HC + H])
        scaled = sb("scaled", [NT, HC + H])
        ev = sb("ev", [P, SLOTS, 2, H])
        ye = sb("ye", [P, SLOTS, H])
        ze = sb("ze", [P, SLOTS, H])
        de = sb("de", [P, SLOTS, H])
        ce = sb("ce", [P, SLOTS, H])
        inv = sb("inv", [NT, H])
        mean_o = sb("mean_o", [NT, HC])
        o = sb("o", [NT, HC])
        act_o = sb("act_o", [NT, HC])
        act_oT = sb("act_oT", [P, KC, NT])
        row1 = sb("row1", [NT, ROW])
        y_out = sb("y_out", [NT, D])

        const_ready, cast_ready = sem("const_ready"), sem("cast_ready")
        w_landed, a_landed = sem("w_landed"), sem("a_landed")
        dst_landed = sem("dst_landed")
        wT_done, wT_copied, wa_done, w_ext_ready = sem("wT_done"), sem("wT_copied"), sem("wa_done"), sem("w_ext_ready")
        b_done = sem("b_done")
        prep_step = sem("prep_step")
        count_ready, rank_done, steps_ready = sem("count_ready"), sem("rank_done"), sem("steps_ready")
        fields_ready, fields_done = sem("fields_ready"), sem("fields_done")
        gathers_begun, aggr_begun, loads_begun = sem("gathers_begun"), sem("aggr_begun"), sem("loads_begun")
        stores_begun = sem("stores_begun")
        x_landed = [sem(f"x_landed{b}") for b in range(2)]
        stats_done = [sem(f"stats_done{b}") for b in range(2)]
        mv_done = [sem(f"mv_done{b}") for b in range(2)]
        sdev_done = [sem(f"sdev_done{b}") for b in range(2)]
        rstd_done = [sem(f"rstd_done{b}") for b in range(2)]
        shift_done = [sem(f"shift_done{b}") for b in range(2)]
        normed = [sem(f"normed{b}") for b in range(2)]
        hnT_done = [sem(f"hnT_done{b}") for b in range(2)]
        hnT_copied = [sem(f"hnT_copied{b}") for b in range(2)]
        rows_done = [sem(f"rows_done{b}") for b in range(2)]
        rows_copied = [sem(f"rows_copied{b}") for b in range(2)]
        rows_stored = [sem(f"rows_stored{b}") for b in range(2)]

        step_sems = ("onehot_ready ends_ready away_ready run_ready max_ready at_end_ready part0_ready rest_ready "
                     "part1_ready marked_ready runs_done "
                     "spread_ready spreadT_done absent_ready seg_sum_ready seg_ready cands_ready newmax_ready own_ready old_ready "
                     "sum_ready logit_ready lpart0_ready lrest_ready lpart1_ready logit_parts_ready fall_ready scale_ready "
                     "edge_done ev_ready z_ready d_ready c_ready w_ready onehot_f_ready begin_ready chosen_ready "
                     "scaled_ready state_moved inv_ready mean_ready o_ready act_ready "
                     "actT_done actT_copied row_done row_copied").split()
        s = {n: sem(n) for n in step_sems}
        for n in "onehotT_done onehotT_copied".split():
            s[n] = [sem(f"{n}{k}") for k in range(2)]
        s["weighted"] = [sem(f"weighted{k}") for k in range(len(PARTS))]
        buffer_sems = "own_read dst_read src_read rows_used x_read".split()
        for n in buffer_sems + "idx_landed self_landed x2_landed lo_landed hi_landed more_landed".split():
            s[n] = [sem(f"{n}{u}") for u in range(NB)]
        stored, dst_copied = sem("stored"), sem("dst_copied")
        from_one = [normed, hnT_done, rows_done, hnT_copied, rows_copied, s["onehotT_done"], s["onehotT_copied"],
                    s["weighted"]] + [s[n] for n in step_sems + buffer_sems]

        block = ctx.enter_context(nc.Block())

        def group_rows(ap, q, size):
            return ap[bass.ds(q * (GROUP * P), size * P), :].rearrange("(t p) c -> p t c", p=P)

        class Step:
            def __init__(self, eng, L, r, rounds_, u):
                self.L, self.u, self.r = L, u, r
                self.i = r + L * (rounds_ + 1) if L else r
                self.k = self.i * NB + u
                snap = (lambda v: v) if isinstance(self.k, int) else eng.snap
                self.k1, self.k2 = snap(self.k + 1), snap(self.k + 2)
                self.half = u % 2

        def pipeline(eng, start, body, finish):
            rounds_ = eng.value_load(rounds[0:1, 0:1], min_val=TILES // NB - 1, max_val=STEPS // NB - 1)
            for L in range(2):
                at = lambda r, j: Step(eng, L, r if j < NB else r + 1, rounds_, j % NB)
                start(at(0, 0))
                body(None, at(0, 0), at(0, 1))
                with eng.Fori(0, rounds_) as r:
                    for j in range(NB):
                        body(at(r, j), at(r, j + 1), at(r, j + 2))
                for j in range(NB - 2):
                    body(at(rounds_, j), at(rounds_, j + 1), at(rounds_, j + 2))
                body(at(rounds_, NB - 2), at(rounds_, NB - 1), None)
                finish(at(rounds_, NB - 1))

        CONSTS, ALL_CONSTS = 11, 15 + NB
        WHOLE, LAST = [P] * GROUP, [P, REST - P]

        @block.sync
        def _(sp):
            sp.dma_start(dst_all, dst.rearrange("(p w) -> p w", p=EP)).then_inc(dst_landed, 16)
            for one in from_one:
                for each in (one if isinstance(one, list) else [one]):
                    nc.sync.sem_inc(each, 1)
            for L, W in enumerate((W0, W1)):
                sp.dma_start(w_in[:, L], W.rearrange("(k p) c -> p k c", p=P)).then_inc(w_landed, 16)

            def load_group(q, i, b, sizes):
                sp.wait_ge(normed[b], i * GROUP + 1)
                if sizes is WHOLE:
                    sp.dma_start(xg[b][:], group_rows(x, q, GROUP)).then_inc(x_landed[b], 16)
                else:
                    r = GROUPS * GROUP * P
                    sp.dma_start(xg[b][:, 0, :], x[r:r + P, :]).then_inc(x_landed[b], 16)
                    sp.dma_start(xg[b][0:sizes[1], 1, :], x[r + P:N, :]).then_inc(x_landed[b], 16)

            with nc.sync.Fori(0, DPAIRS) as i:
                for b in range(2):
                    load_group(i * 2 + b, i, b, WHOLE)
            load_group(GROUPS, DPAIRS, 0, LAST)

            sp.wait_ge(steps_ready, 1)
            sp.wait_ge(stored, 16)
            sp.wait_ge(dst_copied, 16)
            rounds_ = sp.value_load(rounds[0:1, 0:1], min_val=TILES // NB - 1, max_val=STEPS // NB - 1)
            for L in range(2):
                with nc.sync.Fori(0, rounds_ + 1) as r:
                    for u in range(NB):
                        i = r + L * (rounds_ + 1)
                        k = i * NB + u
                        first = sp.value_load(steps_i[0:1, T_EDGE, bass.ds(k, 1)], min_val=0, max_val=E)
                        n = sp.value_load(steps_i[0:1, T_TILE, bass.ds(k, 1)], min_val=0, max_val=TILES - 1)
                        sp.wait_ge(s["src_read"][u], i + 1)
                        sp.wait_ge(s["dst_read"][u], i + 1)
                        nc.sync.sem_inc(loads_begun, 1)
                        for idx, edges in ((src_i[u], src_pad), (dst_i[u], dst_pad)):
                            sp.dma_start(idx[:, 0:IN_RUN],
                                         edges[bass.ds(first, MAIN)].rearrange("(p t) -> p t", t=IN_RUN)
                                         ).then_inc(s["idx_landed"][u], 16)
                            sp.dma_start(idx[:, IN_RUN:SLOTS],
                                         edges[bass.ds(first + MAIN, P)].rearrange("(p t) -> p t", t=1)
                                         ).then_inc(s["idx_landed"][u], 16)
                        if L == 1:
                            sp.wait_ge(s["x_read"][u], r + 1)
                            nc.sync.sem_inc(loads_begun, 1)
                            sp.dma_start(x_row[u][:], x[bass.ds(n * NT, NT), :]).then_inc(s["x2_landed"][u], 16)
                        sp.wait_ge(stored, (rounds_ + 1) * (16 * NB) + 16) if L == 1 else sp.wait_ge(rows_stored[0], 16 * (DPAIRS + 3))
                        sp.wait_ge(rows_stored[1], 16 * (DPAIRS + 1))
                        sp.wait_ge(s["own_read"][u], i + 1)
                        nc.sync.sem_inc(loads_begun, 1)
                        sp.dma_start(self_row[u][:], table[L][bass.ds(n * NT, NT), :]).then_inc(s["self_landed"][u], 16)

        @block.gpsimd
        def _(pool):
            step = [0]

            def link(ins):
                step[0] += 1
                ins.then_inc(const_ready, 1)
                pool.wait_ge(const_ready, step[0])

            link(nc.gpsimd.memset(pad_i[:, 0, :], 0))
            link(nc.gpsimd.memset(pad_i[:, 1, :], 1 << 20))
            pool.dma_start(src_pad[E:E + PAD].rearrange("(p w) -> p w", p=P), pad_i[:, 0, :]).then_inc(rows_stored[0], 16)
            pool.dma_start(dst_pad[E:E + PAD].rearrange("(p w) -> p w", p=P), pad_i[:, 1, :]).then_inc(rows_stored[1], 16)
            for L, bias in enumerate((b0, b1)):
                for j in range(KC):
                    pool.dma_start(b_row[0:1, L, j * P:(j + 1) * P],
                                   bias[j * P:(j + 1) * P].rearrange("(o c) -> o c", o=1)).then_inc(s["more_landed"][L * KC + j], 16)
            link(nc.gpsimd.memset(a_blk[:], 0.0))
            link(nc.gpsimd.memset(ident[:], 0.0))
            link(nc.gpsimd.affine_select(out=ident[:], in_=ident[:], compare_op=ALU.not_equal, fill=1.0, base=0,
                                         pattern=[[-1, P]], channel_multiplier=1))
            link(nc.gpsimd.memset(ones[:], 1.0))
            link(nc.gpsimd.memset(eps[:], 1e-5))
            link(nc.gpsimd.iota(iota_i[:], pattern=[[1, P]], base=0, channel_multiplier=0))
            link(nc.gpsimd.iota(base_i[:], pattern=[[NT, TILES + 1]], base=0, channel_multiplier=0))
            link(nc.gpsimd.memset(reset[:], -BIG))
            link(nc.gpsimd.iota(step_no_i[:], pattern=[[HALF_STEPS, 2]], base=0, channel_multiplier=1))
            assert step[0] == CONSTS
            link(nc.gpsimd.memset(state[:], 0.0))
            link(nc.gpsimd.memset(maxes[:], 0.0))
            link(nc.gpsimd.memset(steps_i[:], 0))
            link(nc.gpsimd.memset(steps[:], 0.0))
            pool.wait_ge(count_ready, 1)
            for u in range(NB):
                link(nc.gpsimd.memset(G[u][:, IN_RUN, :], 0.0))
            assert step[0] == ALL_CONSTS

            def store_group(q, i, b, sizes):
                pool.wait_ge(rows_copied[b], i * GROUP + len(sizes) + 1)
                if sizes is WHOLE:
                    pool.dma_start(group_rows(table[0], q, GROUP), row0[b][:]).then_inc(rows_stored[b], 16)
                else:
                    r = GROUPS * GROUP * P
                    pool.dma_start(table[0][r:r + P, :], row0[b][:, 0, :]).then_inc(rows_stored[b], 16)
                    pool.dma_start(table[0][r + P:N, :], row0[b][0:sizes[1], 1, :]).then_inc(rows_stored[b], 16)

            with nc.gpsimd.Fori(0, DPAIRS) as i:
                for b in range(2):
                    store_group(i * 2 + b, i, b, WHOLE)
            store_group(GROUPS, DPAIRS, 0, LAST)

            pool.wait_ge(steps_ready, 1)
            rounds_ = pool.value_load(rounds[0:1, 0:1], min_val=TILES // NB - 1, max_val=STEPS // NB - 1)
            for L in range(2):
                if L == 0:
                    pool.wait_ge(rows_stored[0], 16 * (DPAIRS + 3))
                    pool.wait_ge(rows_stored[1], 16 * (DPAIRS + 1))
                else:
                    pool.wait_ge(stored, (rounds_ + 1) * (16 * NB) + 16)
                    nc.gpsimd.sem_inc(gathers_begun, 1)
                with nc.gpsimd.Fori(0, rounds_ + 1) as r:
                    for u in range(NB):
                        i = r + L * (rounds_ + 1)
                        more_ = pool.value_load(steps_i[0:1, T_MORE, bass.ds(i * NB + u, 1)], min_val=0, max_val=1)
                        pool.wait_ge(s["rows_used"][u], i + 1)
                        pool.wait_ge(s["idx_landed"][u], i * 64 + 64)
                        nc.gpsimd.sem_inc(gathers_begun, 1)

                        def gather(t, landed):
                            nc.gpsimd.indirect_dma_start(
                                out=G[u][:, t, :], out_offset=None, in_=table[L],
                                in_offset=bass.IndirectOffsetOnAxis(ap=src_i[u][:, t:t + 1], axis=0)).then_inc(landed, 16)

                        for t in range(IN_RUN):
                            gather(t, s["lo_landed" if t < HALF else "hi_landed"][u])
                        with nc.gpsimd.If(more_ > 0):
                            gather(IN_RUN, s["more_landed"][u])

        @block.scalar
        def _(act):
            act.wait_ge(const_ready, 3)
            for L, (a_s, a_d) in enumerate(((a_src0, a_dst0), (a_src1, a_dst1))):
                for k, a in enumerate((a_s, a_d)):
                    for h in range(H):
                        r = h * C % P
                        act.dma_start(a_blk[r:r + C, L, h * C // P, k * H + h:k * H + h + 1],
                                      a[h:h + 1, :].rearrange("o c -> c o")).then_inc(a_landed, 16)
            act.dma_start(src_pad[0:E].rearrange("(p w) -> p w", p=EP), src.rearrange("(p w) -> p w", p=EP)).then_inc(stored, 16)
            act.dma_start(dst_pad[0:E].rearrange("(p w) -> p w", p=EP), dst.rearrange("(p w) -> p w", p=EP)).then_inc(dst_copied, 16)

            def norm_group(i, b, sizes):
                m = len(sizes)
                act.wait_ge(mv_done[b], i + 1)
                nc.scalar.activation(sdev[b][:, 0:m], mv[b][:, 0:m, 1], ACT.Sqrt, bias=eps[:, 0:1]).then_inc(sdev_done[b], 1)
                act.wait_ge(shift_done[b], i + 1)
                act.wait_ge(hnT_done[0], i * GROUP + b * GROUP // 2 + 1)
                act.wait_ge(hnT_done[1], i * GROUP + b * GROUP // 2 + 1)
                for t, r in enumerate(sizes):
                    nc.scalar.activation(hn[b][0:r, t, :], xg[b][0:r, t, :], ACT.Relu,
                                         bias=shift[b][0:r, t:t + 1], scale=rstd[b][0:r, t:t + 1]).then_inc(normed[b], 1)

            def move_rows(i, b, sizes):
                act.wait_ge(rows_stored[b], i * 16 + 16)
                for t, r in enumerate(sizes):
                    act.wait_ge(rows_done[t % 2], i * GROUP + b * GROUP // 2 + t // 2 + 1 + 1)
                    nc.scalar.activation(row0[b][0:r, t, :], bank[3 + t][0:r, 0:ROW], ACT.Identity).then_inc(rows_copied[b], 1)

            norm_group(0, 0, WHOLE)
            with nc.scalar.Fori(0, DPAIRS - 1) as i:
                for b in range(2):
                    norm_group(i + b, 1 - b, WHOLE)
                    move_rows(i, b, WHOLE)
            norm_group(DPAIRS - 1, 1, WHOLE)
            move_rows(DPAIRS - 1, 0, WHOLE)
            norm_group(DPAIRS, 0, LAST)
            move_rows(DPAIRS - 1, 1, WHOLE)
            move_rows(DPAIRS, 0, LAST)

            act.wait_ge(steps_ready, 1)

            def begin_row(t):
                act.wait_ge(s["self_landed"][t.u], t.i * 16 + 16)
                act.wait_ge(s["chosen_ready"], t.k1)
                first = steps[0:NT, F_FIRST, bass.ds(t.k, 1)]
                nc.scalar.activation(begin[t.half][:, HC:HC + H], ones[0:NT, 0:H], ACT.Copy, scale=first)
                nc.scalar.activation(begin[t.half][:, 0:HC], self_row[t.u][:, 0:HC], ACT.Copy, scale=first
                                     ).then_inc(s["begin_ready"], 1)

            def move_onehotT(t):
                act.wait_ge(s["edge_done"], t.k1)
                for f, r in enumerate(range(0, SLOTS, 8)):
                    m = min(8, SLOTS - r)
                    act.wait_ge(s["onehotT_done"][f % 2], t.k * (2 - f % 2) + f // 2 + 2)
                    nc.scalar.activation(onehotT[:, r:r + m, :],
                                         bank[3 + f % 2][0:NT, :].bitcast(BF16)[:, 0:m * P].rearrange("d (t e) -> d t e", e=P),
                                         ACT.Copy).then_inc(s["onehotT_copied"][f % 2], 1)

            def spread_last(t):
                act.wait_ge(s["away_ready"], t.k2)
                act.wait_ge(s["max_ready"], t.k2)
                act.wait_ge(s["spreadT_done"], t.k1)
                for j in range(2):
                    if j == 1:
                        used_ = act.value_load(steps_i[0:1, T_USED, bass.ds(t.k, 1)], min_val=0, max_val=2 * STEPS)
                        act.wait_ge(s["more_landed"][t.u], used_ * 16 + 16)
                    for h in range(H):
                        value = run_max[:, h, IN_RUN - 1:IN_RUN] if j == 0 else G[t.u][:, IN_RUN, HC + h:HC + h + 1]
                        last = nc.scalar.activation(spread[:, j, h, :], away[:, j, :], ACT.Identity, bias=value)
                last.then_inc(s["spread_ready"], 1)

            def widen_onehot(t):
                act.wait_ge(s["onehot_ready"], t.k2)
                nc.scalar.activation(onehot_f[t.half][:], onehot[:], ACT.Copy).then_inc(s["onehot_f_ready"], 1)

            def exponentials(t):
                act.wait_ge(s["fall_ready"], t.k2)
                nc.scalar.activation(scale[t.half][:], fall[:], ACT.Exp).then_inc(s["scale_ready"], 1)
                act.wait_ge(s["c_ready"], t.k2)
                nc.scalar.activation(G[t.u][:, :, HC:HC + H], ce[:], ACT.Exp).then_inc(s["w_ready"], 1)

            def move_state(t):
                act.wait_ge(s["mean_ready"], t.k1)
                act.wait_ge(s["chosen_ready"], t.k2)
                act.wait_ge(s["rows_used"][t.u], t.i + 2)
                nc.scalar.activation(state[:], bank[5][0:NT, 0:HC + H], ACT.Copy).then_inc(s["state_moved"], 1)

            def gelu(t):
                act.wait_ge(s["o_ready"], t.k2)
                if t.L == 0:
                    act.wait_ge(s["actT_done"], t.k1)
                nc.scalar.activation(act_o[:], o[:], ACT.Gelu).then_inc(s["act_ready"], 1)

            def move_actT(t):
                if t.L == 0:
                    act.wait_ge(s["row_done"], t.k1)
                    act.wait_ge(s["actT_done"], t.k2)
                    nc.scalar.activation(act_oT[:], bank[6][:, 0:KC * NT].rearrange("c (k n) -> c k n", n=NT),
                                         ACT.Copy).then_inc(s["actT_copied"], 1)

            def store(t):
                n = act.value_load(steps_i[0:1, T_TILE, bass.ds(t.k, 1)], min_val=0, max_val=TILES - 1)
                if t.L == 0:
                    act.wait_ge(s["row_done"], t.k2)
                    act.wait_ge(stored, t.k * 16 + 16)
                    nc.scalar.activation(row1[:], bank[7][0:NT, 0:ROW], ACT.Copy).then_inc(s["row_copied"], 1)
                    act.wait_ge(s["row_copied"], t.k2)
                    nc.scalar.sem_inc(stores_begun, 1)
                    act.dma_start(table[1][bass.ds(n * NT, NT), :], row1[:]).then_inc(stored, 16)
                else:
                    act.wait_ge(s["x_read"][t.u], t.r + 2)
                    nc.scalar.sem_inc(stores_begun, 1)
                    act.dma_start(out[bass.ds(n * NT, NT), :], y_out[:]).then_inc(stored, 16)

            def act_start(t):
                if t.L == 1:
                    act.wait_ge(s["actT_done"], t.k1)
                begin_row(t)
                move_onehotT(t)
                widen_onehot(t)
                spread_last(t)
                exponentials(t)

            def act_body(before, now, after):
                if after:
                    begin_row(after)
                    move_onehotT(after)
                    widen_onehot(after)
                    spread_last(after)
                if before:
                    gelu(before)
                    move_actT(before)
                if after:
                    exponentials(after)
                move_state(now)
                if before:
                    store(before)

            def act_finish(t):
                gelu(t)
                move_actT(t)
                store(t)

            pipeline(nc.scalar, act_start, act_body, act_finish)
            last = act.value_load(rounds[0:1, 0:1], min_val=TILES // NB - 1, max_val=STEPS // NB - 1)
            act.wait_ge(stored, (last + 1) * (2 * NB * 16) + 16)
            nc.scalar.sem_inc(stores_begun, 1)

        @block.vector
        def _(dve):
            step = [0]

            def link(ins):
                step[0] += 1
                ins.then_inc(prep_step, 1)
                dve.wait_ge(prep_step, step[0])

            dve.wait_ge(const_ready, CONSTS)
            nc.vector.tensor_copy(iota_f[:], iota_i[:])
            nc.vector.tensor_copy(iota_b[:], iota_i[:])
            nc.vector.tensor_copy(step_no[:], step_no_i[:])
            nc.vector.tensor_copy(ident_b[:], ident[:]).then_inc(cast_ready, 1)
            link(nc.vector.tensor_copy(base_f[:], base_i[:]))
            for L in range(2):
                dve.wait_ge(wT_done, L + 1)
                nc.vector.tensor_copy(w_t[:, L], bank[1 + L][:, :].rearrange("p (k c) -> p k c", k=KC)).then_inc(wT_copied, 1)
            dve.wait_ge(w_landed, 32)
            for L in range(2):
                nc.vector.tensor_copy(w_ext[:, L, :, 0:D], w_in[:, L])
            dve.wait_ge(wa_done, 1)
            nc.vector.tensor_copy(w_ext[:, :, :, D:ROW],
                                  bank[0][:, 0:2 * KC * 2 * H].rearrange("p (l k a) -> p l k a", l=2, k=KC)).then_inc(w_ext_ready, 1)
            dve.wait_ge(b_done, 1)
            nc.vector.tensor_copy(b_all[:], bank[7][:, :].rearrange("p (l c) -> p l c", l=2))

            dve.wait_ge(dst_landed, 16)
            link(nc.vector.tensor_copy(samp[:], dst_all.rearrange("p (a s) -> p a s", s=STRIDE)[:, :, 0]))
            link(nc.vector.tensor_tensor(below, wide(samp[:], 1, TILES + 1), wide(base_f[0:EP, :], 2, SAMPLES), ALU.is_lt))
            nc.vector.tensor_reduce(count[:], below, AX.X, ALU.add).then_inc(count_ready, 1)

            def stats_group(i, b, sizes):
                dve.wait_ge(x_landed[b], i * 16 + 16 * (1 if sizes is WHOLE else 2))
                for t, r in enumerate(sizes):
                    last = nc.vector.bn_stats(stats[b][0:r, t, :], xg[b][0:r, t, :])
                last.then_inc(stats_done[b], 1)
                dve.wait_ge(stats_done[b], i + 1)
                nc.vector.sem_inc(aggr_begun, 1)
                for t, r in enumerate(sizes):
                    last = nc.vector.bn_aggr(mv[b][0:r, t, :], stats[b][0:r, t, :])
                last.then_inc(mv_done[b], 1)
                dve.wait_ge(sdev_done[b], i + 1)
                m = len(sizes)
                nc.vector.reciprocal(rstd[b][:, 0:m], sdev[b][:, 0:m]).then_inc(rstd_done[b], 1)
                dve.wait_ge(rstd_done[b], i + 1)
                nc.vector.scalar_tensor_tensor(out=shift[b][:, 0:m], in0=mv[b][:, 0:m, 0], scalar=-1.0,
                                               in1=rstd[b][:, 0:m], op0=ALU.mult, op1=ALU.mult).then_inc(shift_done[b], 1)

            def copy_group(i, b, sizes):
                for t, r in enumerate(sizes):
                    k = t % 2
                    turn = i * GROUP + b * GROUP // 2 + t // 2
                    dve.wait_ge(rows_done[k], turn + 1)
                    dve.wait_ge(hnT_done[k], turn + 1 + 1)
                    nc.vector.tensor_copy(hnT[k][:, :, 0:r], bank[1 + k][:, 0:KC * P].rearrange("c (k n) -> c k n", n=P)[:, :, 0:r]
                                          ).then_inc(hnT_copied[k], 1)

            def find_tiles():
                dve.wait_ge(rank_done, 1)
                link(nc.vector.tensor_copy(rank[:], bank[0][:, 256:256 + TILES + 1]))
                link(nc.vector.tensor_scalar(first_edge[:], rank[:, 0:TILES], -1.0, float(STRIDE), ALU.add, ALU.mult))
                link(nc.vector.tensor_scalar(first_edge[:], first_edge[:], 0.0, None, ALU.max))
                link(nc.vector.tensor_scalar(span[:], rank[:, 1:TILES + 1], float(STRIDE), -1.0, ALU.mult, ALU.add))
                link(nc.vector.tensor_tensor(span[:], span[:], first_edge[:], ALU.subtract))
                link(nc.vector.tensor_scalar(span[:], span[:], 0.0, None, ALU.max))
                link(nc.vector.tensor_copy(span_i[:], span[:]))
                link(nc.vector.tensor_scalar(span_i[:], span_i[:], 7, None, ALU.arith_shift_right))
                link(nc.vector.tensor_copy(full[:], span_i[:]))
                link(nc.vector.tensor_scalar(more[:], full[:], float(IN_RUN), None, ALU.is_ge))
                link(nc.vector.tensor_scalar(span[:], full[:], float(65536 // SLOTS + 1), None, ALU.mult))
                link(nc.vector.tensor_copy(span_i[:], span[:]))
                link(nc.vector.tensor_scalar(span_i[:], span_i[:], 16, None, ALU.arith_shift_right))
                link(nc.vector.tensor_copy(chunks[:], span_i[:]))
                link(nc.vector.tensor_scalar(chunks[:], chunks[:], 1.0, None, ALU.add))
                link(nc.vector.tensor_tensor_scan(upto[:], chunks[:], chunks[:], 0.0, ALU.add, ALU.bypass))
                link(nc.vector.tensor_tensor(prior[:], upto[:], chunks[:], ALU.subtract))

            def list_steps():
                hs = HALF_STEPS
                at_step = wide(step_no[0:hs, :], 2, TILES)
                link(nc.vector.tensor_tensor(pick[:], wide(upto[0:hs, :], 1, 2), at_step, ALU.is_le))
                link(nc.vector.tensor_reduce(tile_of[:], pick[:], AX.X, ALU.add))
                link(nc.vector.tensor_tensor(pick[:], wide(iota_f[0:hs, 0:TILES], 1, 2), wide(tile_of[:], 2, TILES), ALU.is_equal))
                link(nc.vector.tensor_reduce(inside[:], pick[:], AX.X, ALU.add))
                for values, f in ((first_edge, F_EDGE), (more, F_MORE), (prior, F_BASE)):
                    link(nc.vector.tensor_tensor(picked[:], pick[:], wide(values[0:hs, :], 1, 2), ALU.mult))
                    link(nc.vector.tensor_reduce(field[:, f, :], picked[:], AX.X, ALU.add))
                link(nc.vector.tensor_tensor(nth[:], step_no[0:hs, :], field[:, F_BASE, :], ALU.subtract))
                link(nc.vector.scalar_tensor_tensor(out=field[:, F_EDGE, :], in0=nth[:], scalar=float(CHUNK),
                                                    in1=field[:, F_EDGE, :], op0=ALU.mult, op1=ALU.add))
                link(nc.vector.scalar_tensor_tensor(out=field[:, F_EDGE, :], in0=field[:, F_EDGE, :], scalar=-float(E),
                                                    in1=inside[:], op0=ALU.add, op1=ALU.mult))
                link(nc.vector.tensor_scalar(field[:, F_EDGE, :], field[:, F_EDGE, :], float(E), None, ALU.add))
                link(nc.vector.scalar_tensor_tensor(out=field[:, F_FIRST, :], in0=nth[:], scalar=0.0, in1=inside[:],
                                                    op0=ALU.is_equal, op1=ALU.mult))
                link(nc.vector.tensor_scalar(field[:, F_LATER, :], field[:, F_FIRST, :], -1.0, 1.0, ALU.mult, ALU.add))
                link(nc.vector.tensor_scalar(field[:, F_TILE, :], tile_of[:], float(TILES - 1), None, ALU.min))
                nc.vector.tensor_scalar(field[:, F_BASE, :], field[:, F_TILE, :], float(NT), None, ALU.mult).then_inc(fields_ready, 1)
                link(nc.vector.tensor_scalar(quads_f[:], upto[:, TILES - 1:TILES], float(NB - 1), None, ALU.add))
                link(nc.vector.tensor_copy(quads_i[:], quads_f[:]))
                link(nc.vector.tensor_scalar(quads_i[:], quads_i[:], NB.bit_length() - 1, None, ALU.arith_shift_right))
                link(nc.vector.tensor_copy(quads_f[:], quads_i[:]))
                link(nc.vector.tensor_scalar(quads_f[:], quads_f[:], -1.0, None, ALU.add))
                link(nc.vector.tensor_copy(rounds[:], quads_f[:]))

            def spread_steps():
                dve.wait_ge(fields_done, 1)
                dve.wait_ge(const_ready, ALL_CONSTS)
                rounds_ = dve.value_load(rounds[0:1, 0:1], min_val=TILES // NB - 1, max_val=STEPS // NB - 1)
                for L in range(2):
                    for f in range(6):
                        row = bank[f // 2][:, (f % 2) * STEPS:(f % 2 + 1) * STEPS]
                        to = steps[:, f, 0:STEPS] if L == 0 else steps[:, f, bass.ds((rounds_ + 1) * NB, STEPS)]
                        link(nc.vector.tensor_copy(to, row))
                for row, f in ((T_TILE, F_TILE), (T_EDGE, F_EDGE), (T_MORE, F_MORE)):
                    link(nc.vector.tensor_copy(steps_i[:, row, :], steps[:, f, :]))
                for u in range(NB):
                    gathered = steps[:, F_MORE, u::NB]
                    link(nc.vector.tensor_tensor_scan(used[:], gathered, gathered, 0.0, ALU.add, ALU.bypass))
                    link(nc.vector.tensor_copy(steps_i[:, T_USED, u::NB], used[:]))
                nc.vector.tensor_copy(quads_f[:], quads_i[:]).then_inc(steps_ready, 1)

            stats_group(0, 0, WHOLE)
            with nc.vector.Fori(0, DPAIRS - 1) as i:
                for b in range(2):
                    stats_group(i + b, 1 - b, WHOLE)
                    copy_group(i, b, WHOLE)
            stats_group(DPAIRS - 1, 1, WHOLE)
            copy_group(DPAIRS - 1, 0, WHOLE)
            stats_group(DPAIRS, 0, LAST)
            copy_group(DPAIRS - 1, 1, WHOLE)
            copy_group(DPAIRS, 0, LAST)
            find_tiles()
            list_steps()
            spread_steps()

            def onehots(t):
                dve.wait_ge(s["idx_landed"][t.u], t.i * 64 + 64)
                nc.vector.tensor_scalar(dloc[:], dst_i[t.u][:], steps[:, F_BASE, bass.ds(t.k, 1)], None, ALU.subtract
                                        ).then_inc(s["dst_read"][t.u], 1)
                dve.wait_ge(s["onehot_f_ready"], t.k1)
                dve.wait_ge(s["runs_done"], t.k1)
                dve.wait_ge(s["dst_read"][t.u], t.i + 2)
                nc.vector.tensor_tensor(onehot[:], wide(iota_b[:, 0:NT], 1, SLOTS), wide(dloc[:], 2, NT), ALU.is_equal
                                        ).then_inc(s["onehot_ready"], 1)
                nc.vector.tensor_tensor(ends[:], dloc[:, 0:IN_RUN - 1], dloc[:, 1:IN_RUN], ALU.not_equal
                                        ).then_inc(s["ends_ready"], 1)
                dve.wait_ge(s["ends_ready"], t.k2)
                nc.vector.tensor_scalar(reset[:, :, 1:IN_RUN], wide(ends[:], 1, H), -BIG, None, ALU.mult)
                dve.wait_ge(s["onehot_ready"], t.k2)
                dve.wait_ge(s["spread_ready"], t.k1)
                nc.vector.tensor_scalar(away[:], onehot[:, IN_RUN - 1:SLOTS, :], -1.0, BIG, ALU.add, ALU.mult
                                        ).then_inc(s["away_ready"], 1)

            def run_maxima(t):
                dve.wait_ge(s["lo_landed"][t.u], t.i * (16 * HALF) + 16 * HALF)
                dve.wait_ge(s["hi_landed"][t.u], t.i * (16 * HALF) + 16 * HALF)
                nc.vector.tensor_copy(a_run[:], G[t.u][:, 0:IN_RUN, HC:HC + H].rearrange("p t h -> p h t")
                                      ).then_inc(s["run_ready"], 1)
                dve.wait_ge(s["away_ready"], t.k2)
                dve.wait_ge(s["run_ready"], t.k2)
                nc.vector.tensor_tensor_scan(run_max[:].rearrange("p h t -> p (h t)"), reset[:].rearrange("p h t -> p (h t)"),
                                             a_run[:].rearrange("p h t -> p (h t)"), 0.0, ALU.add, ALU.max
                                             ).then_inc(s["max_ready"], 1)
                dve.wait_ge(s["max_ready"], t.k2)
                nc.vector.tensor_tensor(at_end[:], run_max[:, :, 0:IN_RUN - 1].rearrange("p h t -> p t h"),
                                        wide(ends[:], 2, H), ALU.mult).then_inc(s["at_end_ready"], 1)
                nc.vector.tensor_copy(marked[:, :, 3 * H], ends[:])
                dve.wait_ge(s["at_end_ready"], t.k2)
                nc.vector.tensor_copy(marked[:, :, 0:H], at_end[:]).then_inc(s["part0_ready"], 1)
                dve.wait_ge(s["part0_ready"], t.k2)
                nc.vector.tensor_tensor(at_end_r[:], at_end[:], marked[:, :, 0:H], ALU.subtract).then_inc(s["rest_ready"], 1)
                dve.wait_ge(s["rest_ready"], t.k2)
                nc.vector.tensor_copy(marked[:, :, H:2 * H], at_end_r[:]).then_inc(s["part1_ready"], 1)
                dve.wait_ge(s["part1_ready"], t.k2)
                nc.vector.tensor_tensor(marked[:, :, 2 * H:3 * H], at_end_r[:], marked[:, :, H:2 * H], ALU.subtract
                                        ).then_inc(s["marked_ready"], 1)

            def tile_maxima(t):
                dve.wait_ge(s["runs_done"], t.k2)
                runs = bank[0][0:NT, 0:(IN_RUN - 1) * (3 * H + 1)].rearrange("d (t a) -> d t a", a=3 * H + 1)
                nc.vector.tensor_scalar(absent[:], runs[:, :, 3 * H], -1.0, BIG, ALU.add, ALU.mult).then_inc(s["absent_ready"], 1)
                for h in range(H):
                    last = nc.vector.tensor_reduce(seg_sum[:, h, :], runs[:, :, h:3 * H:H], AX.X, ALU.add)
                last.then_inc(s["seg_sum_ready"], 1)
                dve.wait_ge(s["absent_ready"], t.k2)
                dve.wait_ge(s["seg_sum_ready"], t.k2)
                nc.vector.tensor_tensor(seg[:], seg_sum[:], wide(absent[:], 1, H), ALU.add).then_inc(s["seg_ready"], 1)
                dve.wait_ge(s["seg_ready"], t.k2)
                nc.vector.tensor_reduce(cands[:, :, 0], seg[:], AX.X, ALU.max)
                dve.wait_ge(s["self_landed"][t.u], t.i * 16 + 16)
                nc.vector.tensor_scalar(own[:], self_row[t.u][:, HC:HC + H], steps[0:NT, F_FIRST, bass.ds(t.k, 1)], None, ALU.mult
                                        ).then_inc(s["own_ready"], 1)
                dve.wait_ge(s["own_ready"], t.k2)
                nc.vector.scalar_tensor_tensor(out=maxes[:, 0, :], in0=maxes[:, 1, :], scalar=steps[0:NT, F_LATER, bass.ds(t.k, 1)],
                                               in1=own[:], op0=ALU.mult, op1=ALU.add).then_inc(s["old_ready"], 1)
                dve.wait_ge(s["old_ready"], t.k2)
                nc.vector.tensor_copy(cands[:, :, 3], maxes[:, 0, :])
                dve.wait_ge(s["spreadT_done"], t.k2)
                for j in range(2):
                    last = nc.vector.tensor_reduce(cands[:, :, 1 + j], bank[1 + j][0:NT, :].rearrange("d (h e) -> d h e", e=P),
                                                   AX.X, ALU.max)
                last.then_inc(s["cands_ready"], 1)
                dve.wait_ge(s["cands_ready"], t.k2)
                nc.vector.tensor_reduce(maxes[:, 1, :], cands[:], AX.X, ALU.max).then_inc(s["newmax_ready"], 1)
                dve.wait_ge(s["newmax_ready"], t.k2)
                nc.vector.tensor_tensor(summed[:], maxes[:], wide(self_row[t.u][:, HC + H:ROW], 1, 2), ALU.add).then_inc(s["sum_ready"], 1)
                dve.wait_ge(s["begin_ready"], t.k2)
                nc.vector.tensor_copy(logit[:, 2, :], self_row[t.u][:, HC + H:ROW]).then_inc(s["own_read"][t.u], 1)
                dve.wait_ge(s["sum_ready"], t.k2)
                dve.wait_ge(s["scale_ready"], t.k1)
                nc.vector.scalar_tensor_tensor(out=logit[:, 0:2, :], in0=summed[:], scalar=0.2, in1=summed[:],
                                               op0=ALU.mult, op1=ALU.max).then_inc(s["logit_ready"], 1)
                dve.wait_ge(s["logit_ready"], t.k2)
                nc.vector.tensor_tensor(fall[:], logit[:, 0, :], logit[:, 1, :], ALU.subtract).then_inc(s["fall_ready"], 1)
                nc.vector.tensor_copy(logit_p[:, 0], logit[:, 1:3, :]).then_inc(s["lpart0_ready"], 1)
                dve.wait_ge(s["lpart0_ready"], t.k2)
                nc.vector.tensor_tensor(logit_r[:], logit[:, 1:3, :], logit_p[:, 0], ALU.subtract).then_inc(s["lrest_ready"], 1)
                dve.wait_ge(s["lrest_ready"], t.k2)
                nc.vector.tensor_copy(logit_p[:, 1], logit_r[:]).then_inc(s["lpart1_ready"], 1)
                dve.wait_ge(s["lpart1_ready"], t.k2)
                nc.vector.tensor_tensor(logit_p[:, 2], logit_r[:], logit_p[:, 1], ALU.subtract).then_inc(s["logit_parts_ready"], 1)

            def edge_logits(t):
                dve.wait_ge(s["edge_done"], t.k2)
                nc.vector.tensor_reduce(ev[:].rearrange("p t k h -> p t (k h)"),
                                        bank[1][:, 0:SLOTS * 6 * H].rearrange("p (t q a) -> p t a q", q=3, a=2 * H),
                                        AX.X, ALU.add).then_inc(s["ev_ready"], 1)
                used_ = dve.value_load(steps_i[0:1, T_USED, bass.ds(t.k, 1)], min_val=0, max_val=2 * STEPS)
                dve.wait_ge(s["more_landed"][t.u], used_ * 16 + 16)
                dve.wait_ge(s["ev_ready"], t.k2)
                nc.vector.tensor_tensor(ye[:], G[t.u][:, :, HC:HC + H], ev[:, :, 1, :], ALU.add).then_inc(s["src_read"][t.u], 1)
                dve.wait_ge(s["src_read"][t.u], t.i + 2)
                nc.vector.scalar_tensor_tensor(out=ze[:], in0=ye[:], scalar=0.2, in1=ye[:], op0=ALU.mult, op1=ALU.max
                                               ).then_inc(s["z_ready"], 1)
                dve.wait_ge(s["z_ready"], t.k2)
                nc.vector.tensor_tensor(de[:], ze[:], ev[:, :, 0, :], ALU.subtract).then_inc(s["d_ready"], 1)
                dve.wait_ge(s["d_ready"], t.k2)
                nc.vector.tensor_scalar(ce[:], de[:], 0.0, None, ALU.min).then_inc(s["c_ready"], 1)

            def weigh(t, part):
                t0, t1 = PARTS[part]
                dve.wait_ge(s["w_ready"], t.k2)
                rows = G[t.u][:, t0:t1, 0:HC].rearrange("p t (h c) -> p t h c", h=H)
                nc.vector.tensor_tensor(rows, rows, wide(G[t.u][:, t0:t1, HC:HC + H], 3, C), ALU.mult
                                        ).then_inc(s["weighted"][part], 1)

            def scale_state(t):
                dve.wait_ge(s["begin_ready"], t.k2)
                dve.wait_ge(s["state_moved"], t.k1)
                nc.vector.scalar_tensor_tensor(out=chosen[:], in0=state[:], scalar=steps[0:NT, F_LATER, bass.ds(t.k, 1)],
                                               in1=begin[t.half][:], op0=ALU.mult, op1=ALU.add).then_inc(s["chosen_ready"], 1)
                dve.wait_ge(s["scale_ready"], t.k2)
                dve.wait_ge(s["chosen_ready"], t.k2)
                nc.vector.tensor_tensor(scaled[:, 0:HC].rearrange("d (h c) -> d h c", h=H),
                                        chosen[:, 0:HC].rearrange("d (h c) -> d h c", h=H), wide(scale[t.half][:], 2, C), ALU.mult)
                nc.vector.tensor_tensor(scaled[:, HC:HC + H], chosen[:, HC:HC + H], scale[t.half][:], ALU.mult
                                        ).then_inc(s["scaled_ready"], 1)

            def mean(t):
                dve.wait_ge(s["state_moved"], t.k2)
                nc.vector.reciprocal(inv[:], state[:, HC:HC + H]).then_inc(s["inv_ready"], 1)
                dve.wait_ge(s["inv_ready"], t.k2)
                nc.vector.tensor_tensor(mean_o[:].rearrange("d (h c) -> d h c", h=H),
                                        state[:, 0:HC].rearrange("d (h c) -> d h c", h=H), wide(inv[:], 2, C), ALU.mult
                                        ).then_inc(s["mean_ready"], 1)
                dve.wait_ge(s["mean_ready"], t.k2)
                dve.wait_ge(s["act_ready"], t.k1)
                nc.vector.tensor_tensor(o[:], mean_o[:], b_all[0:NT, t.L, :], ALU.add).then_inc(s["o_ready"], 1)

            def residual(t):
                if t.L == 1:
                    dve.wait_ge(s["x2_landed"][t.u], t.r * 16 + 16)
                    dve.wait_ge(s["act_ready"], t.k2)
                    dve.wait_ge(stored, t.k * 16 + 16)
                    nc.vector.tensor_tensor(y_out[:], act_o[:], x_row[t.u][:], ALU.add).then_inc(s["x_read"][t.u], 1)

            def dve_start(t):
                onehots(t)
                run_maxima(t)
                tile_maxima(t)
                edge_logits(t)

            def dve_body(before, now, after):
                weigh(now, 0)
                if after:
                    onehots(after)
                weigh(now, 1)
                if before:
                    mean(before)
                if after:
                    run_maxima(after)
                weigh(now, 2)
                weigh(now, 3)
                scale_state(now)
                if after:
                    tile_maxima(after)
                if before:
                    residual(before)
                if after:
                    edge_logits(after)

            def dve_finish(t):
                mean(t)
                residual(t)

            pipeline(nc.vector, dve_start, dve_body, dve_finish)

        @block.tensor
        def _(pe):
            pe.wait_ge(const_ready, CONSTS)
            pe.wait_ge(w_landed, 32)
            for L in range(2):
                for k in range(KC):
                    for j in range(KC):
                        last = nc.tensor.transpose(bank[1 + L][:, k * D + j * P:k * D + (j + 1) * P],
                                                   w_in[:, L, j, k * P:(k + 1) * P], ident[:])
                last.then_inc(wT_done, 1)
            for u in range(2 * KC):
                pe.wait_ge(s["more_landed"][u], 16)
            nc.tensor.matmul(bank[7][:, :], ones[0:1, :], b_row[0:1, :, :].rearrange("o l c -> o (l c)"),
                             start=True, stop=True).then_inc(b_done, 1)
            pe.wait_ge(a_landed, 16 * 4 * H)
            pe.wait_ge(wT_copied, 2)
            for L in range(2):
                for j in range(KC):
                    for k in range(KC):
                        o0 = (L * KC + j) * 2 * H
                        last = nc.tensor.matmul(bank[0][:, o0:o0 + 2 * H], w_t[:, L, k, j * P:(j + 1) * P],
                                                a_blk[:, L, k, :], start=(k == 0), stop=(k == KC - 1))
            last.then_inc(wa_done, 1)
            pe.wait_ge(count_ready, 1)
            nc.tensor.matmul(bank[0][:, 256:256 + TILES + 1], ones[0:EP, :], count[:], start=True, stop=True).then_inc(rank_done, 1)
            pe.wait_ge(w_ext_ready, 1)
            pe.wait_ge(cast_ready, 1)

            def dense_group(i, b, sizes):
                for t, r in enumerate(sizes):
                    k = t % 2
                    turn = i * GROUP + b * GROUP // 2 + t // 2
                    pe.wait_ge(hnT_copied[k], turn + 1)
                    pe.wait_ge(normed[b], i * GROUP + t + 1 + 1)
                    for j in range(KC):
                        last = nc.tensor.transpose(bank[1 + k][:, j * P:j * P + r], hn[b][0:r, t, j * P:(j + 1) * P], ident[0:r, 0:r])
                    last.then_inc(hnT_done[k], 1)
                    pe.wait_ge(rows_copied[1 - b], (i + b) * GROUP + 1)
                    pe.wait_ge(hnT_copied[k], turn + 1 + 1)
                    for j in range(KC):
                        last = nc.tensor.matmul(bank[3 + t][0:r, 0:ROW], hnT[k][:, j, 0:r], w_ext[:, 0, j, :],
                                                start=(j == 0), stop=(j == KC - 1))
                    last.then_inc(rows_done[k], 1)

            with nc.tensor.Fori(0, DPAIRS) as i:
                for b in range(2):
                    dense_group(i, b, WHOLE)
            dense_group(DPAIRS, 0, LAST)

            pe.wait_ge(fields_ready, 1)
            pe.wait_ge(rows_copied[0], DPAIRS * GROUP + len(LAST) + 1)
            pe.wait_ge(rows_copied[1], DPAIRS * GROUP + 1)
            for f in range(6):
                for j in range(2):
                    at = (f % 2) * STEPS + j * HALF_STEPS
                    last = nc.tensor.matmul(bank[f // 2][:, at:at + HALF_STEPS], field[:, f, j:j + 1].broadcast_to([HALF_STEPS, P]),
                                            ident[0:HALF_STEPS, 0:HALF_STEPS], start=True, stop=True)
            last.then_inc(fields_done, 1)
            pe.wait_ge(steps_ready, 1)

            def transpose_onehot(t):
                pe.wait_ge(s["onehot_ready"], t.k2)
                for f, r in enumerate(range(0, SLOTS, 8)):
                    pe.wait_ge(s["onehotT_copied"][f % 2], t.k * (2 - f % 2) + f // 2 + 1)
                    to = bank[3 + f % 2][0:NT, :].bitcast(BF16)
                    for j in range(r, min(r + 8, SLOTS)):
                        last = nc.tensor.transpose(to[:, (j - r) * P:(j - r + 1) * P], onehot[:, j, :], ident_b[:])
                    last.then_inc(s["onehotT_done"][f % 2], 1)

            def runs_to_nodes(t):
                pe.wait_ge(s["marked_ready"], t.k2)
                w = 3 * H + 1
                for j in range(IN_RUN - 1):
                    last = nc.tensor.matmul(bank[0][0:NT, j * w:(j + 1) * w], onehot[:, j, :], marked[:, j, :], start=True, stop=True)
                last.then_inc(s["runs_done"], 1)

            def last_to_nodes(t):
                pe.wait_ge(s["spread_ready"], t.k2)
                for j in range(2):
                    for h in range(H):
                        last = nc.tensor.transpose(bank[1 + j][0:NT, h * P:(h + 1) * P], spread[:, j, h, :], ident[:])
                last.then_inc(s["spreadT_done"], 1)

            def logits_to_edges(t):
                pe.wait_ge(s["onehotT_copied"][0], t.k * 2 + 3)
                pe.wait_ge(s["onehotT_copied"][1], t.k2)
                pe.wait_ge(s["logit_parts_ready"], t.k2)
                w = 3 * 2 * H
                for j in range(SLOTS):
                    last = nc.tensor.matmul(bank[1][:, j * w:(j + 1) * w], onehotT[:, j, :],
                                            logit_p[:].rearrange("d q k h -> d (q k h)"), start=True, stop=True)
                last.then_inc(s["edge_done"], 1)

            def sum_up(t, part):
                t0, t1 = PARTS[part]
                if part == 0:
                    pe.wait_ge(s["onehot_f_ready"], t.k2)
                    pe.wait_ge(s["state_moved"], t.k1)
                pe.wait_ge(s["weighted"][part], t.k2)
                for j in range(t0, t1):
                    last = nc.tensor.matmul(bank[5][0:NT, 0:HC + H], onehot_f[t.half][:, j, :], G[t.u][:, j, 0:HC + H],
                                            start=(j == 0), stop=False)
                if part == len(PARTS) - 1:
                    pe.wait_ge(s["scaled_ready"], t.k2)
                    nc.tensor.matmul(bank[5][0:NT, 0:HC + H], ident[0:NT, 0:NT], scaled[:], start=False, stop=True
                                     ).then_inc(s["rows_used"][t.u], 1)

            def transpose_act(t):
                if t.L == 0:
                    pe.wait_ge(s["act_ready"], t.k2)
                    for j in range(KC):
                        last = nc.tensor.transpose(bank[6][:, j * NT:(j + 1) * NT], act_o[:, j * P:(j + 1) * P], ident[0:NT, 0:NT])
                    last.then_inc(s["actT_done"], 1)

            def next_rows(t):
                if t.L == 0:
                    pe.wait_ge(s["row_copied"], t.k1)
                    pe.wait_ge(s["actT_copied"], t.k2)
                    for j in range(KC):
                        last = nc.tensor.matmul(bank[7][0:NT, 0:ROW], act_oT[:, j, :], w_ext[:, 1, j, :],
                                                start=(j == 0), stop=(j == KC - 1))
                    last.then_inc(s["row_done"], 1)

            def pe_start(t):
                transpose_onehot(t)
                runs_to_nodes(t)
                last_to_nodes(t)
                logits_to_edges(t)

            def pe_body(before, now, after):
                sum_up(now, 0)
                if after:
                    transpose_onehot(after)
                sum_up(now, 1)
                if after:
                    runs_to_nodes(after)
                    last_to_nodes(after)
                sum_up(now, 2)
                if before:
                    transpose_act(before)
                if after:
                    logits_to_edges(after)
                sum_up(now, 3)
                if before:
                    next_rows(before)

            def pe_finish(t):
                transpose_act(t)
                next_rows(t)

            pipeline(nc.tensor, pe_start, pe_body, pe_finish)


_INS = ["x", "src", "dst", "edge_attr_32", "L0_gnn_W0", "L0_gnn_a_src0", "L0_gnn_a_dst0", "L0_gnn_b0",
        "L0_gnn_W1", "L0_gnn_a_src1", "L0_gnn_a_dst1", "L0_gnn_b1"]
_OUTS = [((12500, 256), "float32")]


def kernel(**inputs):
    import numpy as _np
    import concourse.bacc as _bacc
    from concourse import mybir as _mybir
    from concourse.bass_utils import run_bass_kernel_spmd as _run

    nc = _bacc.Bacc("TRN2", target_bir_lowering=False, num_devices=1)
    arrays, args = {}, []
    for name in _INS:
        a = _np.ascontiguousarray(inputs[name])
        arrays[f"in_{name}_dram"] = a
        args.append(nc.dram_tensor(f"in_{name}_dram", a.shape, _mybir.dt.from_np(a.dtype), kind="ExternalInput").ap())
    for i, (shape, dtype) in enumerate(_OUTS):
        dt = _mybir.dt.from_np(_np.dtype(dtype))
        args.append(nc.dram_tensor(f"out_{i}_dram", shape, dt, kind="ExternalOutput").ap())
    two_layer_graph_attention(nc, *args)
    r = _run(nc, [arrays], core_ids=[0])
    got = tuple(r.results[0][f"out_{i}_dram"] for i in range(len(_OUTS)))
    return got[0]
```

```python
from contextlib import ExitStack

import concourse.bass as bass
from concourse import mybir

ALU = mybir.AluOpType
ACT = mybir.ActivationFunctionType
AX = mybir.AxisListType
F32 = mybir.dt.float32
BF16 = mybir.dt.bfloat16
I32 = mybir.dt.int32

P = 128
BIG = 1.0e30


def wide(ap, axis, n):
    shape = list(ap.shape)
    return ap.unsqueeze(axis).broadcast_to(shape[:axis] + [n] + shape[axis:])


def two_layer_graph_attention(nc, x, src, dst, edge_attr, W0, a_src0, a_dst0, b0, W1, a_src1, a_dst1, b1, out):
    N, D = x.shape
    E = src.shape[0]
    H, C = a_src0.shape
    HC = H * C
    ROW = HC + 2 * H
    KC = D // P

    NT = 125
    TILES = N // NT
    PAIRS = TILES // 2
    IN_RUN = E // TILES // P + 1
    SLOTS = IN_RUN + 1
    CHUNK = SLOTS * P
    MAIN = IN_RUN * P
    HALF = IN_RUN // 2
    STRIDE = 16
    EP = 125
    EW = E // EP
    SAMPLES = EW // STRIDE
    PAD = CHUNK + P
    NB = 4
    STEPS = -(-(TILES + (E + TILES * 2 * STRIDE) // CHUNK) // NB) * NB
    HALF_STEPS = STEPS // 2
    PARTS = [(0, 3), (3, 8), (8, 14), (14, SLOTS)]
    assert TILES % NB == 0 and E % (EP * STRIDE) == 0 and D == HC and KC == 2 and IN_RUN == 16

    GROUP = 4
    GROUPS = N // (GROUP * P)
    REST = N - GROUPS * GROUP * P
    XB = 4
    TURNS = GROUPS // XB
    assert GROUPS % XB == 0 and P < REST <= 2 * P

    with ExitStack() as ctx:
        def sb(name, shape, dt=F32):
            return ctx.enter_context(nc.sbuf_tensor(name, shape, dt))

        def sem(name):
            return ctx.enter_context(nc.semaphore(name))

        def dram(name, shape, dt):
            return nc.dram_tensor(name, shape, dt, kind="Internal").ap()

        table = [dram("table0", [N, ROW], F32), dram("table1", [N, ROW], F32)]
        src_pad = dram("src_pad", [E + PAD], I32)
        dst_pad = dram("dst_pad", [E + PAD], I32)

        bank = [ctx.enter_context(nc.psum_tensor(f"bank{i}", [P, 512], F32)) for i in range(8)]

        rows_all = sb("rows_all", [P, NB, SLOTS, ROW])
        G = [rows_all[:, u] for u in range(NB)]
        spare = rows_all[0:EP].rearrange("p u t c -> p (u t c)")
        dst_all = spare[:, 0:EW].bitcast(I32)
        below = spare[:, EW:EW + -(-(TILES + 1) * SAMPLES // 2)].bitcast(BF16).rearrange("p (n a) -> p n a", a=SAMPLES)

        ident = sb("ident", [P, P])
        ones = sb("ones", [P, P])
        iota_i = sb("iota_i", [P, P], I32)
        iota_f = sb("iota_f", [P, P])
        iota_b = sb("iota_b", [P, P], BF16)
        ident_b = sb("ident_b", [P, P], BF16)
        base_i = sb("base_i", [P, TILES + 1], I32)
        base_f = sb("base_f", [P, TILES + 1])
        eps = sb("eps", [P, 1])
        w_in = sb("w_in", [P, 2, KC, D])
        w_t = sb("w_t", [P, 2, KC, D])
        a_blk = sb("a_blk", [P, 2, KC, 2 * H])
        w_ext = sb("w_ext", [P, 2, KC, ROW])
        b_row = sb("b_row", [1, 2, HC])
        pad_i = sb("pad_i", [P, 2, PAD // P], I32)

        samp = sb("samp", [EP, SAMPLES])
        count = sb("count", [EP, TILES + 1])
        rank = sb("rank", [P, TILES + 1])
        first_edge = sb("first_edge", [P, TILES])
        span = sb("span", [P, TILES])
        span_i = sb("span_i", [P, TILES], I32)
        full = sb("full", [P, TILES])
        more = sb("more", [P, TILES])
        chunks = sb("chunks", [P, TILES])
        upto = sb("upto", [P, TILES])
        prior = sb("prior", [P, TILES])
        step_no = sb("step_no", [P, 2])
        step_no_i = sb("step_no_i", [P, 2], I32)
        pick = sb("pick", [HALF_STEPS, 2, TILES])
        picked = sb("picked", [HALF_STEPS, 2, TILES])
        tile_of = sb("tile_of", [HALF_STEPS, 2])
        inside = sb("inside", [HALF_STEPS, 2])
        nth = sb("nth", [HALF_STEPS, 2])
        F_TILE, F_BASE, F_EDGE, F_MORE, F_FIRST, F_LATER = range(6)
        field = sb("field", [HALF_STEPS, 6, 2])
        steps = sb("steps", [P, 6, 2 * STEPS])
        T_TILE, T_EDGE, T_MORE, T_USED = range(4)
        steps_i = sb("steps_i", [P, 4, 2 * STEPS], I32)
        quads_f = sb("quads_f", [P, 1])
        quads_i = sb("quads_i", [P, 1], I32)
        rounds = sb("rounds", [P, 1], I32)
        used = sb("used", [P, 2 * STEPS // NB])

        xg = [sb(f"xg{b}", [P, GROUP, D]) for b in range(XB)]
        hn = [sb(f"hn{b}", [P, GROUP, D]) for b in range(2)]
        stats = [sb(f"stats{b}", [P, GROUP, 6]) for b in range(2)]
        mv = [sb(f"mv{b}", [P, GROUP, 2]) for b in range(2)]
        sdev = [sb(f"sdev{b}", [P, GROUP]) for b in range(2)]
        rstd = [sb(f"rstd{b}", [P, GROUP]) for b in range(2)]
        shift = [sb(f"shift{b}", [P, GROUP]) for b in range(2)]
        hnT = [sb(f"hnT{b}", [P, KC, P]) for b in range(2)]
        row0 = [sb(f"row0{b}", [P, GROUP, ROW]) for b in range(2)]

        src_i = [sb(f"src_i{u}", [P, SLOTS], I32) for u in range(NB)]
        dst_i = [sb(f"dst_i{u}", [P, SLOTS], I32) for u in range(NB)]
        self_row = [sb(f"self_row{u}", [NT, ROW]) for u in range(NB)]
        x_row = [sb(f"x_row{u}", [NT, D]) for u in range(NB)]
        dloc = sb("dloc", [P, SLOTS], BF16)
        onehot = sb("onehot", [P, SLOTS, NT], BF16)
        onehot_f = [sb(f"onehot_f{k}", [P, SLOTS, NT]) for k in range(2)]
        onehotT = sb("onehotT", [NT, SLOTS, P], BF16)
        ends = sb("ends", [P, IN_RUN - 1])
        reset = sb("reset", [P, H, IN_RUN])
        away = sb("away", [P, 2, NT])
        a_run = sb("a_run", [P, H, IN_RUN])
        run_max = sb("run_max", [P, H, IN_RUN])
        at_end = sb("at_end", [P, IN_RUN - 1, H])
        at_end_r = sb("at_end_r", [P, IN_RUN - 1, H])
        marked = sb("marked", [P, IN_RUN - 1, 3 * H + 1], BF16)
        spread = sb("spread", [P, 2, H, NT])
        absent = sb("absent", [NT, IN_RUN - 1])
        seg_sum = sb("seg_sum", [NT, H, IN_RUN - 1])
        seg = sb("seg", [NT, H, IN_RUN - 1])
        own = sb("own", [NT, H])
        cands = sb("cands", [NT, H, 5])
        OLD, NEW = 3, 4
        summed = sb("summed", [NT, 2, H])
        logit = sb("logit", [NT, 3, H])
        logit_r = sb("logit_r", [NT, 2, H])
        logit_p = sb("logit_p", [NT, 3, 2, H], BF16)
        fall = sb("fall", [NT, H])
        scale = sb("scale", [NT, H])
        keep = [sb(f"keep{k}", [NT, H]) for k in range(2)]
        begin = [sb(f"begin{k}", [NT, HC + H]) for k in range(2)]
        state = sb("state", [NT, HC + H])
        scaled = sb("scaled", [NT, HC + H])
        ev = sb("ev", [P, SLOTS, 2, H])
        ye = sb("ye", [P, SLOTS, H])
        ze = sb("ze", [P, SLOTS, H])
        de = sb("de", [P, SLOTS, H])
        ce = sb("ce", [P, SLOTS, H])
        inv = sb("inv", [NT, H])
        mean_o = sb("mean_o", [NT, HC])
        act_o = sb("act_o", [NT, HC])
        act_oT = sb("act_oT", [P, KC, NT])
        row1 = sb("row1", [NT, ROW])
        y_out = sb("y_out", [NT, D])

        const_ready, cast_ready = sem("const_ready"), sem("cast_ready")
        w_landed, a_landed = sem("w_landed"), sem("a_landed")
        dst_landed = sem("dst_landed")
        wT_done, wT_copied, wa_done, w_ext_ready = sem("wT_done"), sem("wT_copied"), sem("wa_done"), sem("w_ext_ready")
        prep_step = sem("prep_step")
        count_ready, rank_done, steps_ready = sem("count_ready"), sem("rank_done"), sem("steps_ready")
        fields_ready, fields_done = sem("fields_ready"), sem("fields_done")
        gathers_begun, aggr_begun, loads_begun = sem("gathers_begun"), sem("aggr_begun"), sem("loads_begun")
        stores_begun = sem("stores_begun")
        x_landed = [sem(f"x_landed{b}") for b in range(XB)]
        stats_done = [sem(f"stats_done{b}") for b in range(2)]
        mv_done = [sem(f"mv_done{b}") for b in range(2)]
        sdev_done = [sem(f"sdev_done{b}") for b in range(2)]
        rstd_done = [sem(f"rstd_done{b}") for b in range(2)]
        shift_done = [sem(f"shift_done{b}") for b in range(2)]
        normed = [sem(f"normed{b}") for b in range(2)]
        hnT_done = [sem(f"hnT_done{b}") for b in range(2)]
        hnT_copied = [sem(f"hnT_copied{b}") for b in range(2)]
        rows_done = [sem(f"rows_done{b}") for b in range(2)]
        rows_copied = [sem(f"rows_copied{b}") for b in range(2)]
        rows_stored = [sem(f"rows_stored{b}") for b in range(2)]

        step_sems = ("onehot_lo_ready onehot_ready ends_ready reset_ready away_ready run_ready max_ready at_end_ready part0_ready rest_ready "
                     "part1_ready marked_ready runs_done "
                     "spread_ready spreadT_done absent_ready seg_sum_ready seg_ready cands_ready newmax_ready own_ready old_ready "
                     "sum_ready logit_ready lpart0_ready lrest_ready lpart1_ready logit_parts_ready fall_ready scale_ready "
                     "edge_done ev_ready z_ready d_ready c_ready w_ready onehot_f_ready shares_ready alpha_ready "
                     "scaled_ready state_moved inv_ready mean_ready o_done act_ready "
                     "actT_done actT_copied row_done row_copied").split()
        s = {n: sem(n) for n in step_sems}
        for n in "onehotT_done onehotT_copied".split():
            s[n] = [sem(f"{n}{k}") for k in range(2)]
        s["weighted"] = [sem(f"weighted{k}") for k in range(len(PARTS))]
        buffer_sems = "own_read dst_read src_read rows_used x_read".split()
        for n in buffer_sems + "idx_landed self_landed x2_landed lo_landed hi_landed more_landed".split():
            s[n] = [sem(f"{n}{u}") for u in range(NB)]
        stored, dst_copied = sem("stored"), sem("dst_copied")
        from_one = [normed, hnT_done, rows_done, hnT_copied, rows_copied, s["onehotT_done"], s["onehotT_copied"],
                    s["weighted"]] + [s[n] for n in step_sems + buffer_sems]

        block = ctx.enter_context(nc.Block())

        def group_rows(ap, q, size):
            return ap[bass.ds(q * (GROUP * P), size * P), :].rearrange("(t p) c -> p t c", p=P)

        class Group:
            def __init__(self, i, j):
                self.i, self.j = i, j
                self.q = i * XB + j
                self.xb, self.turn = j % XB, i + j // XB
                self.b, self.n = j % 2, i * (XB // 2) + j // 2
                self.last = isinstance(self.q, int) and self.q == GROUPS
                self.sizes = LAST if self.last else WHOLE

        class Step:
            def __init__(self, eng, L, r, rounds_, u):
                self.L, self.u, self.r = L, u, r
                self.i = r + L * (rounds_ + 1) if L else r
                self.k = self.i * NB + u
                snap = (lambda v: v) if isinstance(self.k, int) else eng.snap
                self.k1, self.k2 = snap(self.k + 1), snap(self.k + 2)
                self.half = u % 2

        def pipeline(eng, start, body, finish):
            rounds_ = eng.value_load(rounds[0:1, 0:1], min_val=TILES // NB - 1, max_val=STEPS // NB - 1)
            for L in range(2):
                at = lambda r, j: Step(eng, L, r if j < NB else r + 1, rounds_, j % NB)
                start(at(0, 0))
                body(None, None, at(0, 0), at(0, 1))
                body(None, at(0, 0), at(0, 1), at(0, 2))
                with eng.Fori(0, rounds_) as r:
                    for j in range(NB):
                        body(at(r, j), at(r, j + 1), at(r, j + 2), at(r, j + 3))
                body(at(rounds_, 0), at(rounds_, 1), at(rounds_, 2), at(rounds_, 3))
                body(at(rounds_, 1), at(rounds_, 2), at(rounds_, 3), None)
                finish(at(rounds_, 2), at(rounds_, 3))

        O_AT = KC * NT
        CONSTS, ALL_CONSTS = 11, 15 + NB
        WHOLE, LAST = [P] * GROUP, [P, REST - P]

        @block.sync
        def _(sp):
            sp.dma_start(dst_all, dst.rearrange("(p w) -> p w", p=EP)).then_inc(dst_landed, 16)
            for one in from_one:
                for each in (one if isinstance(one, list) else [one]):
                    nc.sync.sem_inc(each, 1)
            for L, W in enumerate((W0, W1)):
                sp.dma_start(w_in[:, L], W.rearrange("(k p) c -> p k c", p=P)).then_inc(w_landed, 16)

            def load_group(g):
                if not g.last:
                    sp.dma_start(xg[g.xb][:], group_rows(x, g.q, GROUP)).then_inc(x_landed[g.xb], 16)
                else:
                    r = GROUPS * GROUP * P
                    sp.dma_start(xg[g.xb][:, 0, :], x[r:r + P, :]).then_inc(x_landed[g.xb], 16)
                    sp.dma_start(xg[g.xb][0:g.sizes[1], 1, :], x[r + P:N, :]).then_inc(x_landed[g.xb], 16)

            for j in range(XB):
                load_group(Group(0, j))
            with nc.sync.Fori(0, TURNS - 1) as i:
                for j in range(XB):
                    sp.wait_ge(normed[j % 2], (i * (XB // 2) + j // 2) * GROUP + GROUP + 1)
                    load_group(Group(i, XB + j))
            sp.wait_ge(normed[0], (TURNS - 1) * (XB // 2) * GROUP + GROUP + 1)
            load_group(Group(TURNS, 0))

            sp.wait_ge(steps_ready, 1)
            sp.wait_ge(stored, 16)
            sp.wait_ge(dst_copied, 16)
            rounds_ = sp.value_load(rounds[0:1, 0:1], min_val=TILES // NB - 1, max_val=STEPS // NB - 1)
            for L in range(2):
                with nc.sync.Fori(0, rounds_ + 1) as r:
                    for u in range(NB):
                        i = r + L * (rounds_ + 1)
                        k = i * NB + u
                        first = sp.value_load(steps_i[0:1, T_EDGE, bass.ds(k, 1)], min_val=0, max_val=E)
                        n = sp.value_load(steps_i[0:1, T_TILE, bass.ds(k, 1)], min_val=0, max_val=TILES - 1)
                        sp.wait_ge(s["src_read"][u], i + 1)
                        sp.wait_ge(s["dst_read"][u], i + 1)
                        nc.sync.sem_inc(loads_begun, 1)
                        for idx, edges in ((src_i[u], src_pad), (dst_i[u], dst_pad)):
                            sp.dma_start(idx[:, 0:IN_RUN],
                                         edges[bass.ds(first, MAIN)].rearrange("(p t) -> p t", t=IN_RUN)
                                         ).then_inc(s["idx_landed"][u], 16)
                            sp.dma_start(idx[:, IN_RUN:SLOTS],
                                         edges[bass.ds(first + MAIN, P)].rearrange("(p t) -> p t", t=1)
                                         ).then_inc(s["idx_landed"][u], 16)
                        if L == 1:
                            sp.wait_ge(s["x_read"][u], r + 1)
                            nc.sync.sem_inc(loads_begun, 1)
                            sp.dma_start(x_row[u][:], x[bass.ds(n * NT, NT), :]).then_inc(s["x2_landed"][u], 16)
                        sp.wait_ge(stored, (rounds_ + 1) * (16 * NB) + 16) if L == 1 else sp.wait_ge(rows_stored[0], 16 * (GROUPS // 2 + 3))
                        sp.wait_ge(rows_stored[1], 16 * (GROUPS // 2 + 1))
                        sp.wait_ge(s["own_read"][u], i + 1)
                        nc.sync.sem_inc(loads_begun, 1)
                        sp.dma_start(self_row[u][:], table[L][bass.ds(n * NT, NT), :]).then_inc(s["self_landed"][u], 16)

        @block.gpsimd
        def _(pool):
            step = [0]

            def link(ins):
                step[0] += 1
                ins.then_inc(const_ready, 1)
                pool.wait_ge(const_ready, step[0])

            link(nc.gpsimd.memset(pad_i[:, 0, :], 0))
            link(nc.gpsimd.memset(pad_i[:, 1, :], 1 << 20))
            pool.dma_start(src_pad[E:E + PAD].rearrange("(p w) -> p w", p=P), pad_i[:, 0, :]).then_inc(rows_stored[0], 16)
            pool.dma_start(dst_pad[E:E + PAD].rearrange("(p w) -> p w", p=P), pad_i[:, 1, :]).then_inc(rows_stored[1], 16)
            for L, bias in enumerate((b0, b1)):
                for j in range(KC):
                    pool.dma_start(b_row[0:1, L, j * P:(j + 1) * P],
                                   bias[j * P:(j + 1) * P].rearrange("(o c) -> o c", o=1)).then_inc(s["more_landed"][L * KC + j], 16)
            link(nc.gpsimd.memset(a_blk[:], 0.0))
            link(nc.gpsimd.memset(ident[:], 0.0))
            link(nc.gpsimd.affine_select(out=ident[:], in_=ident[:], compare_op=ALU.not_equal, fill=1.0, base=0,
                                         pattern=[[-1, P]], channel_multiplier=1))
            link(nc.gpsimd.memset(ones[:], 1.0))
            link(nc.gpsimd.memset(eps[:], 1e-5))
            link(nc.gpsimd.iota(iota_i[:], pattern=[[1, P]], base=0, channel_multiplier=0))
            link(nc.gpsimd.iota(base_i[:], pattern=[[NT, TILES + 1]], base=0, channel_multiplier=0))
            link(nc.gpsimd.memset(reset[:], -BIG))
            link(nc.gpsimd.iota(step_no_i[:], pattern=[[HALF_STEPS, 2]], base=0, channel_multiplier=1))
            assert step[0] == CONSTS
            link(nc.gpsimd.memset(state[:], 0.0))
            link(nc.gpsimd.memset(cands[:], 0.0))
            link(nc.gpsimd.memset(steps_i[:], 0))
            link(nc.gpsimd.memset(steps[:], 0.0))
            pool.wait_ge(count_ready, 1)
            for u in range(NB):
                link(nc.gpsimd.memset(G[u][:, IN_RUN, :], 0.0))
            assert step[0] == ALL_CONSTS

            def store_group(g):
                pool.wait_ge(rows_copied[g.b], g.n * GROUP + len(g.sizes) + 1)
                if not g.last:
                    pool.dma_start(group_rows(table[0], g.q, GROUP), row0[g.b][:]).then_inc(rows_stored[g.b], 16)
                else:
                    r = GROUPS * GROUP * P
                    pool.dma_start(table[0][r:r + P, :], row0[g.b][:, 0, :]).then_inc(rows_stored[g.b], 16)
                    pool.dma_start(table[0][r + P:N, :], row0[g.b][0:g.sizes[1], 1, :]).then_inc(rows_stored[g.b], 16)

            with nc.gpsimd.Fori(0, TURNS) as i:
                for j in range(XB):
                    store_group(Group(i, j))
            store_group(Group(TURNS, 0))

            pool.wait_ge(steps_ready, 1)
            rounds_ = pool.value_load(rounds[0:1, 0:1], min_val=TILES // NB - 1, max_val=STEPS // NB - 1)
            for L in range(2):
                if L == 0:
                    pool.wait_ge(rows_stored[0], 16 * (GROUPS // 2 + 3))
                    pool.wait_ge(rows_stored[1], 16 * (GROUPS // 2 + 1))
                else:
                    pool.wait_ge(stored, (rounds_ + 1) * (16 * NB) + 16)
                    nc.gpsimd.sem_inc(gathers_begun, 1)
                with nc.gpsimd.Fori(0, rounds_ + 1) as r:
                    for u in range(NB):
                        i = r + L * (rounds_ + 1)
                        more_ = pool.value_load(steps_i[0:1, T_MORE, bass.ds(i * NB + u, 1)], min_val=0, max_val=1)
                        pool.wait_ge(s["rows_used"][u], i + 1)
                        pool.wait_ge(s["idx_landed"][u], i * 64 + 64)
                        nc.gpsimd.sem_inc(gathers_begun, 1)

                        def gather(t, landed):
                            nc.gpsimd.indirect_dma_start(
                                out=G[u][:, t, :], out_offset=None, in_=table[L],
                                in_offset=bass.IndirectOffsetOnAxis(ap=src_i[u][:, t:t + 1], axis=0)).then_inc(landed, 16)

                        for t in range(IN_RUN):
                            gather(t, s["lo_landed" if t < HALF else "hi_landed"][u])
                        with nc.gpsimd.If(more_ > 0):
                            gather(IN_RUN, s["more_landed"][u])

        @block.scalar
        def _(act):
            act.wait_ge(const_ready, 3)
            for L, (a_s, a_d) in enumerate(((a_src0, a_dst0), (a_src1, a_dst1))):
                for k, a in enumerate((a_s, a_d)):
                    for h in range(H):
                        r = h * C % P
                        act.dma_start(a_blk[r:r + C, L, h * C // P, k * H + h:k * H + h + 1],
                                      a[h:h + 1, :].rearrange("o c -> c o")).then_inc(a_landed, 16)
            act.dma_start(src_pad[0:E].rearrange("(p w) -> p w", p=EP), src.rearrange("(p w) -> p w", p=EP)).then_inc(stored, 16)
            act.dma_start(dst_pad[0:E].rearrange("(p w) -> p w", p=EP), dst.rearrange("(p w) -> p w", p=EP)).then_inc(dst_copied, 16)

            def norm_group(g):
                m = len(g.sizes)
                act.wait_ge(mv_done[g.b], g.n + 1)
                nc.scalar.activation(sdev[g.b][:, 0:m], mv[g.b][:, 0:m, 1], ACT.Sqrt, bias=eps[:, 0:1]).then_inc(sdev_done[g.b], 1)
                act.wait_ge(shift_done[g.b], g.n + 1)
                if g.j > 1 or not isinstance(g.i, int):
                    for k in range(2):
                        act.wait_ge(hnT_done[k], g.i * (XB // 2 * GROUP) + (g.j // 2 - 1) * GROUP + (g.b + 1) * GROUP // 2 + 1)
                for t, r in enumerate(g.sizes):
                    nc.scalar.activation(hn[g.b][0:r, t, :], xg[g.xb][0:r, t, :], ACT.Relu,
                                         bias=shift[g.b][0:r, t:t + 1], scale=rstd[g.b][0:r, t:t + 1]).then_inc(normed[g.b], 1)

            def move_rows(g):
                act.wait_ge(rows_stored[g.b], g.n * 16 + 16)
                for t, r in enumerate(g.sizes):
                    act.wait_ge(rows_done[t % 2], g.n * GROUP + g.b * GROUP // 2 + t // 2 + 1 + 1)
                    nc.scalar.activation(row0[g.b][0:r, t, :], bank[3 + t][0:r, 0:ROW], ACT.Identity).then_inc(rows_copied[g.b], 1)

            norm_group(Group(0, 0))
            with nc.scalar.Fori(0, TURNS - 1) as i:
                for j in range(XB):
                    norm_group(Group(i, j + 1))
                    move_rows(Group(i, j))
            for j in range(XB):
                norm_group(Group(TURNS - 1, j + 1))
                move_rows(Group(TURNS - 1, j))
            move_rows(Group(TURNS, 0))

            act.wait_ge(steps_ready, 1)

            def own_alpha(t):
                act.wait_ge(s["self_landed"][t.u], t.i * 16 + 16)
                act.wait_ge(s["logit_parts_ready"], t.k1)
                nc.scalar.activation(logit[:, 2, :], self_row[t.u][:, HC + H:ROW], ACT.Copy).then_inc(s["alpha_ready"], 1)

            def move_onehotT(t):
                act.wait_ge(s["edge_done"], t.k1)
                for f, r in enumerate(range(0, SLOTS, 8)):
                    m = min(8, SLOTS - r)
                    act.wait_ge(s["onehotT_done"][f % 2], t.k * (2 - f % 2) + f // 2 + 2)
                    nc.scalar.activation(onehotT[:, r:r + m, :],
                                         bank[3 + f % 2][0:NT, :].bitcast(BF16)[:, 0:m * P].rearrange("d (t e) -> d t e", e=P),
                                         ACT.Copy).then_inc(s["onehotT_copied"][f % 2], 1)

            def spread_last(t):
                act.wait_ge(s["away_ready"], t.k2)
                act.wait_ge(s["max_ready"], t.k2)
                act.wait_ge(s["spreadT_done"], t.k1)
                for j in range(2):
                    if j == 1:
                        used_ = act.value_load(steps_i[0:1, T_USED, bass.ds(t.k, 1)], min_val=0, max_val=2 * STEPS)
                        act.wait_ge(s["more_landed"][t.u], used_ * 16 + 16)
                    for h in range(H):
                        value = run_max[:, h, IN_RUN - 1:IN_RUN] if j == 0 else G[t.u][:, IN_RUN, HC + h:HC + h + 1]
                        last = nc.scalar.activation(spread[:, j, h, :], away[:, j, :], ACT.Identity, bias=value)
                last.then_inc(s["spread_ready"], 1)

            def widen_onehot(t):
                act.wait_ge(s["onehot_ready"], t.k2)
                nc.scalar.activation(onehot_f[t.half][:], onehot[:], ACT.Copy).then_inc(s["onehot_f_ready"], 1)

            def exponentials(t):
                act.wait_ge(s["fall_ready"], t.k2)
                nc.scalar.activation(scale[:], fall[:], ACT.Exp).then_inc(s["scale_ready"], 1)
                act.wait_ge(s["c_ready"], t.k2)
                nc.scalar.activation(G[t.u][:, :, HC:HC + H], ce[:], ACT.Exp).then_inc(s["w_ready"], 1)

            def begin_row(t):
                act.wait_ge(s["scale_ready"], t.k2)
                nc.scalar.activation(begin[t.half][:, HC:HC + H], scale[:], ACT.Copy, scale=steps[0:NT, F_FIRST, bass.ds(t.k, 1)])
                nc.scalar.activation(keep[t.half][:], scale[:], ACT.Copy, scale=steps[0:NT, F_LATER, bass.ds(t.k, 1)]
                                     ).then_inc(s["shares_ready"], 1)
                act.wait_ge(s["shares_ready"], t.k2)
                for h in range(H):
                    last = nc.scalar.activation(begin[t.half][:, h * C:(h + 1) * C], self_row[t.u][:, h * C:(h + 1) * C],
                                                ACT.Copy, scale=begin[t.half][:, HC + h:HC + h + 1])
                last.then_inc(s["own_read"][t.u], 1)

            def move_state(t):
                act.wait_ge(s["mean_ready"], t.k1)
                act.wait_ge(s["rows_used"][t.u], t.i + 2)
                nc.scalar.activation(state[:], bank[5][0:NT, 0:HC + H], ACT.Copy).then_inc(s["state_moved"], 1)

            def gelu(t):
                act.wait_ge(s["o_done"], t.k2)
                if t.L == 0:
                    act.wait_ge(s["actT_done"], t.k1)
                nc.scalar.activation(act_o[:], bank[6][0:NT, O_AT:O_AT + HC], ACT.Gelu).then_inc(s["act_ready"], 1)

            def move_actT(t):
                if t.L == 0:
                    act.wait_ge(s["row_done"], t.k1)
                    act.wait_ge(s["actT_done"], t.k2)
                    nc.scalar.activation(act_oT[:], bank[6][:, 0:KC * NT].rearrange("c (k n) -> c k n", n=NT),
                                         ACT.Copy).then_inc(s["actT_copied"], 1)

            def store(t):
                n = act.value_load(steps_i[0:1, T_TILE, bass.ds(t.k, 1)], min_val=0, max_val=TILES - 1)
                if t.L == 0:
                    act.wait_ge(s["row_done"], t.k2)
                    act.wait_ge(stored, t.k * 16 + 16)
                    nc.scalar.activation(row1[:], bank[7][0:NT, 0:ROW], ACT.Copy).then_inc(s["row_copied"], 1)
                    act.wait_ge(s["row_copied"], t.k2)
                    nc.scalar.sem_inc(stores_begun, 1)
                    act.dma_start(table[1][bass.ds(n * NT, NT), :], row1[:]).then_inc(stored, 16)
                else:
                    act.wait_ge(s["x_read"][t.u], t.r + 2)
                    nc.scalar.sem_inc(stores_begun, 1)
                    act.dma_start(out[bass.ds(n * NT, NT), :], y_out[:]).then_inc(stored, 16)

            def act_start(t):
                if t.L == 1:
                    act.wait_ge(s["actT_done"], t.k1)
                move_onehotT(t)
                widen_onehot(t)
                own_alpha(t)
                spread_last(t)
                exponentials(t)
                begin_row(t)

            def act_body(earlier, before, now, after):
                if after:
                    move_onehotT(after)
                    own_alpha(after)
                    spread_last(after)
                if before:
                    gelu(before)
                if after:
                    widen_onehot(after)
                if earlier:
                    store(earlier)
                if before:
                    move_actT(before)
                if after:
                    exponentials(after)
                move_state(now)
                if after:
                    begin_row(after)

            def act_finish(earlier, t):
                store(earlier)
                gelu(t)
                move_actT(t)
                store(t)

            pipeline(nc.scalar, act_start, act_body, act_finish)
            last = act.value_load(rounds[0:1, 0:1], min_val=TILES // NB - 1, max_val=STEPS // NB - 1)
            act.wait_ge(stored, (last + 1) * (2 * NB * 16) + 16)
            nc.scalar.sem_inc(stores_begun, 1)

        @block.vector
        def _(dve):
            step = [0]

            def link(ins):
                step[0] += 1
                ins.then_inc(prep_step, 1)
                dve.wait_ge(prep_step, step[0])

            dve.wait_ge(const_ready, CONSTS)
            nc.vector.tensor_copy(iota_f[:], iota_i[:])
            nc.vector.tensor_copy(iota_b[:], iota_i[:])
            nc.vector.tensor_copy(step_no[:], step_no_i[:])
            nc.vector.tensor_copy(ident_b[:], ident[:]).then_inc(cast_ready, 1)
            link(nc.vector.tensor_copy(base_f[:], base_i[:]))
            for L in range(2):
                dve.wait_ge(wT_done, L + 1)
                nc.vector.tensor_copy(w_t[:, L], bank[1 + L][:, :].rearrange("p (k c) -> p k c", k=KC)).then_inc(wT_copied, 1)
            dve.wait_ge(w_landed, 32)
            for L in range(2):
                nc.vector.tensor_copy(w_ext[:, L, :, 0:D], w_in[:, L])
            dve.wait_ge(wa_done, 1)
            nc.vector.tensor_copy(w_ext[:, :, :, D:ROW],
                                  bank[0][:, 0:2 * KC * 2 * H].rearrange("p (l k a) -> p l k a", l=2, k=KC)).then_inc(w_ext_ready, 1)

            dve.wait_ge(dst_landed, 16)
            link(nc.vector.tensor_copy(samp[:], dst_all.rearrange("p (a s) -> p a s", s=STRIDE)[:, :, 0]))
            link(nc.vector.tensor_tensor(below, wide(samp[:], 1, TILES + 1), wide(base_f[0:EP, :], 2, SAMPLES), ALU.is_lt))
            nc.vector.tensor_reduce(count[:], below, AX.X, ALU.add).then_inc(count_ready, 1)

            def stats_group(g):
                dve.wait_ge(x_landed[g.xb], g.turn * 16 + 16 * (2 if g.last else 1))
                for t, r in enumerate(g.sizes):
                    last = nc.vector.bn_stats(stats[g.b][0:r, t, :], xg[g.xb][0:r, t, :])
                last.then_inc(stats_done[g.b], 1)
                dve.wait_ge(stats_done[g.b], g.n + 1)
                nc.vector.sem_inc(aggr_begun, 1)
                for t, r in enumerate(g.sizes):
                    last = nc.vector.bn_aggr(mv[g.b][0:r, t, :], stats[g.b][0:r, t, :])
                last.then_inc(mv_done[g.b], 1)

            def scales_group(g):
                dve.wait_ge(sdev_done[g.b], g.n + 1)
                m = len(g.sizes)
                nc.vector.reciprocal(rstd[g.b][:, 0:m], sdev[g.b][:, 0:m]).then_inc(rstd_done[g.b], 1)
                dve.wait_ge(rstd_done[g.b], g.n + 1)
                nc.vector.scalar_tensor_tensor(out=shift[g.b][:, 0:m], in0=mv[g.b][:, 0:m, 0], scalar=-1.0,
                                               in1=rstd[g.b][:, 0:m], op0=ALU.mult, op1=ALU.mult).then_inc(shift_done[g.b], 1)

            def copy_tile(g, t):
                k = t % 2
                turn = g.n * GROUP + g.b * GROUP // 2 + t // 2
                dve.wait_ge(rows_done[k], turn + 1)
                dve.wait_ge(hnT_done[k], turn + 1 + 1)
                nc.vector.tensor_copy(hnT[k][:, :, 0:g.sizes[t]],
                                      bank[1 + k][:, 0:KC * P].rearrange("c (k n) -> c k n", n=P)[:, :, 0:g.sizes[t]]
                                      ).then_inc(hnT_copied[k], 1)

            def find_tiles():
                dve.wait_ge(rank_done, 1)
                link(nc.vector.tensor_copy(rank[:], bank[0][:, 256:256 + TILES + 1]))
                link(nc.vector.tensor_scalar(first_edge[:], rank[:, 0:TILES], -1.0, float(STRIDE), ALU.add, ALU.mult))
                link(nc.vector.tensor_scalar(first_edge[:], first_edge[:], 0.0, None, ALU.max))
                link(nc.vector.tensor_scalar(span[:], rank[:, 1:TILES + 1], float(STRIDE), -1.0, ALU.mult, ALU.add))
                link(nc.vector.tensor_tensor(span[:], span[:], first_edge[:], ALU.subtract))
                link(nc.vector.tensor_scalar(span[:], span[:], 0.0, None, ALU.max))
                link(nc.vector.tensor_copy(span_i[:], span[:]))
                link(nc.vector.tensor_scalar(span_i[:], span_i[:], 7, None, ALU.arith_shift_right))
                link(nc.vector.tensor_copy(full[:], span_i[:]))
                link(nc.vector.tensor_scalar(more[:], full[:], float(IN_RUN), None, ALU.is_ge))
                link(nc.vector.tensor_scalar(span[:], full[:], float(65536 // SLOTS + 1), None, ALU.mult))
                link(nc.vector.tensor_copy(span_i[:], span[:]))
                link(nc.vector.tensor_scalar(span_i[:], span_i[:], 16, None, ALU.arith_shift_right))
                link(nc.vector.tensor_copy(chunks[:], span_i[:]))
                link(nc.vector.tensor_scalar(chunks[:], chunks[:], 1.0, None, ALU.add))
                link(nc.vector.tensor_tensor_scan(upto[:], chunks[:], chunks[:], 0.0, ALU.add, ALU.bypass))
                link(nc.vector.tensor_tensor(prior[:], upto[:], chunks[:], ALU.subtract))

            def list_steps():
                hs = HALF_STEPS
                at_step = wide(step_no[0:hs, :], 2, TILES)
                link(nc.vector.tensor_tensor(pick[:], wide(upto[0:hs, :], 1, 2), at_step, ALU.is_le))
                link(nc.vector.tensor_reduce(tile_of[:], pick[:], AX.X, ALU.add))
                link(nc.vector.tensor_tensor(pick[:], wide(iota_f[0:hs, 0:TILES], 1, 2), wide(tile_of[:], 2, TILES), ALU.is_equal))
                link(nc.vector.tensor_reduce(inside[:], pick[:], AX.X, ALU.add))
                for values, f in ((first_edge, F_EDGE), (more, F_MORE), (prior, F_BASE)):
                    link(nc.vector.tensor_tensor(picked[:], pick[:], wide(values[0:hs, :], 1, 2), ALU.mult))
                    link(nc.vector.tensor_reduce(field[:, f, :], picked[:], AX.X, ALU.add))
                link(nc.vector.tensor_tensor(nth[:], step_no[0:hs, :], field[:, F_BASE, :], ALU.subtract))
                link(nc.vector.scalar_tensor_tensor(out=field[:, F_EDGE, :], in0=nth[:], scalar=float(CHUNK),
                                                    in1=field[:, F_EDGE, :], op0=ALU.mult, op1=ALU.add))
                link(nc.vector.scalar_tensor_tensor(out=field[:, F_EDGE, :], in0=field[:, F_EDGE, :], scalar=-float(E),
                                                    in1=inside[:], op0=ALU.add, op1=ALU.mult))
                link(nc.vector.tensor_scalar(field[:, F_EDGE, :], field[:, F_EDGE, :], float(E), None, ALU.add))
                link(nc.vector.scalar_tensor_tensor(out=field[:, F_FIRST, :], in0=nth[:], scalar=0.0, in1=inside[:],
                                                    op0=ALU.is_equal, op1=ALU.mult))
                link(nc.vector.tensor_scalar(field[:, F_LATER, :], field[:, F_FIRST, :], -1.0, 1.0, ALU.mult, ALU.add))
                link(nc.vector.tensor_scalar(field[:, F_TILE, :], tile_of[:], float(TILES - 1), None, ALU.min))
                nc.vector.tensor_scalar(field[:, F_BASE, :], field[:, F_TILE, :], float(NT), None, ALU.mult).then_inc(fields_ready, 1)
                link(nc.vector.tensor_scalar(quads_f[:], upto[:, TILES - 1:TILES], float(NB - 1), None, ALU.add))
                link(nc.vector.tensor_copy(quads_i[:], quads_f[:]))
                link(nc.vector.tensor_scalar(quads_i[:], quads_i[:], NB.bit_length() - 1, None, ALU.arith_shift_right))
                link(nc.vector.tensor_copy(quads_f[:], quads_i[:]))
                link(nc.vector.tensor_scalar(quads_f[:], quads_f[:], -1.0, None, ALU.add))
                link(nc.vector.tensor_copy(rounds[:], quads_f[:]))

            def spread_steps():
                dve.wait_ge(fields_done, 1)
                dve.wait_ge(const_ready, ALL_CONSTS)
                rounds_ = dve.value_load(rounds[0:1, 0:1], min_val=TILES // NB - 1, max_val=STEPS // NB - 1)
                for L in range(2):
                    for f in range(6):
                        row = bank[f // 2][:, (f % 2) * STEPS:(f % 2 + 1) * STEPS]
                        to = steps[:, f, 0:STEPS] if L == 0 else steps[:, f, bass.ds((rounds_ + 1) * NB, STEPS)]
                        link(nc.vector.tensor_copy(to, row))
                for row, f in ((T_TILE, F_TILE), (T_EDGE, F_EDGE), (T_MORE, F_MORE)):
                    link(nc.vector.tensor_copy(steps_i[:, row, :], steps[:, f, :]))
                for u in range(NB):
                    gathered = steps[:, F_MORE, u::NB]
                    link(nc.vector.tensor_tensor_scan(used[:], gathered, gathered, 0.0, ALU.add, ALU.bypass))
                    link(nc.vector.tensor_copy(steps_i[:, T_USED, u::NB], used[:]))
                nc.vector.tensor_copy(quads_f[:], quads_i[:]).then_inc(steps_ready, 1)

            def between(g, after):
                copy_tile(g, 0)
                stats_group(after)
                copy_tile(g, 1)
                scales_group(after)
                for t in range(2, GROUP):
                    copy_tile(g, t)

            stats_group(Group(0, 0))
            scales_group(Group(0, 0))
            with nc.vector.Fori(0, TURNS - 1) as i:
                for j in range(XB):
                    between(Group(i, j), Group(i, j + 1))
            for j in range(XB):
                between(Group(TURNS - 1, j), Group(TURNS - 1, j + 1))
            for t in range(len(LAST)):
                copy_tile(Group(TURNS, 0), t)
            find_tiles()
            list_steps()
            spread_steps()

            def onehots(t):
                dve.wait_ge(s["idx_landed"][t.u], t.i * 64 + 64)
                nc.vector.tensor_scalar(dloc[:], dst_i[t.u][:], steps[:, F_BASE, bass.ds(t.k, 1)], None, ALU.subtract
                                        ).then_inc(s["dst_read"][t.u], 1)
                dve.wait_ge(s["onehot_f_ready"], t.k1)
                dve.wait_ge(s["runs_done"], t.k1)
                dve.wait_ge(s["dst_read"][t.u], t.i + 2)
                for t0, t1, ready in ((0, 8, "onehot_lo_ready"), (8, SLOTS, "onehot_ready")):
                    nc.vector.tensor_tensor(onehot[:, t0:t1, :], wide(iota_b[:, 0:NT], 1, t1 - t0), wide(dloc[:, t0:t1], 2, NT),
                                            ALU.is_equal).then_inc(s[ready], 1)
                nc.vector.tensor_tensor(ends[:], dloc[:, 0:IN_RUN - 1], dloc[:, 1:IN_RUN], ALU.not_equal
                                        ).then_inc(s["ends_ready"], 1)
                dve.wait_ge(s["onehot_ready"], t.k2)
                dve.wait_ge(s["spread_ready"], t.k1)
                nc.vector.tensor_scalar(away[:], onehot[:, IN_RUN - 1:SLOTS, :], -1.0, BIG, ALU.add, ALU.mult
                                        ).then_inc(s["away_ready"], 1)
                dve.wait_ge(s["ends_ready"], t.k2)
                nc.vector.tensor_scalar(reset[:, :, 1:IN_RUN], wide(ends[:], 1, H), -BIG, None, ALU.mult
                                        ).then_inc(s["reset_ready"], 1)

            def run_maxima(t, done):
                dve.wait_ge(s["lo_landed"][t.u], t.i * (16 * HALF) + 16 * HALF)
                dve.wait_ge(s["hi_landed"][t.u], t.i * (16 * HALF) + 16 * HALF)
                nc.vector.tensor_copy(a_run[:], G[t.u][:, 0:IN_RUN, HC:HC + H].rearrange("p t h -> p h t")
                                      ).then_inc(s["run_ready"], 1)
                mean_weight(done)
                dve.wait_ge(s["reset_ready"], t.k2)
                dve.wait_ge(s["run_ready"], t.k2)
                nc.vector.tensor_tensor_scan(run_max[:].rearrange("p h t -> p (h t)"), reset[:].rearrange("p h t -> p (h t)"),
                                             a_run[:].rearrange("p h t -> p (h t)"), 0.0, ALU.add, ALU.max
                                             ).then_inc(s["max_ready"], 1)
                nc.vector.tensor_copy(marked[:, :, 3 * H], ends[:])
                dve.wait_ge(s["max_ready"], t.k2)
                nc.vector.tensor_tensor(at_end[:], run_max[:, :, 0:IN_RUN - 1].rearrange("p h t -> p t h"),
                                        wide(ends[:], 2, H), ALU.mult).then_inc(s["at_end_ready"], 1)
                mean_product(done)
                dve.wait_ge(s["at_end_ready"], t.k2)
                nc.vector.tensor_copy(marked[:, :, 0:H], at_end[:]).then_inc(s["part0_ready"], 1)
                dve.wait_ge(s["part0_ready"], t.k2)
                nc.vector.tensor_tensor(at_end_r[:], at_end[:], marked[:, :, 0:H], ALU.subtract).then_inc(s["rest_ready"], 1)
                dve.wait_ge(s["rest_ready"], t.k2)
                nc.vector.tensor_copy(marked[:, :, H:2 * H], at_end_r[:]).then_inc(s["part1_ready"], 1)
                dve.wait_ge(s["self_landed"][t.u], t.i * 16 + 16)
                nc.vector.tensor_scalar(own[:], self_row[t.u][:, HC:HC + H], steps[0:NT, F_FIRST, bass.ds(t.k, 1)], None, ALU.mult
                                        ).then_inc(s["own_ready"], 1)
                dve.wait_ge(s["part1_ready"], t.k2)
                nc.vector.tensor_tensor(marked[:, :, 2 * H:3 * H], at_end_r[:], marked[:, :, H:2 * H], ALU.subtract
                                        ).then_inc(s["marked_ready"], 1)
                dve.wait_ge(s["own_ready"], t.k2)
                nc.vector.scalar_tensor_tensor(out=cands[:, :, OLD], in0=cands[:, :, NEW], scalar=steps[0:NT, F_LATER, bass.ds(t.k, 1)],
                                               in1=own[:], op0=ALU.mult, op1=ALU.add).then_inc(s["old_ready"], 1)

            def tile_maxima(t, now):
                dve.wait_ge(s["runs_done"], t.k2)
                runs = bank[0][0:NT, 0:(IN_RUN - 1) * (3 * H + 1)].rearrange("d (t a) -> d t a", a=3 * H + 1)
                nc.vector.tensor_scalar(absent[:], runs[:, :, 3 * H], -1.0, BIG, ALU.add, ALU.mult).then_inc(s["absent_ready"], 1)
                nc.vector.tensor_reduce(seg_sum[:], runs[:, :, 0:3 * H].rearrange("d t (q h) -> d h t q", h=H), AX.X, ALU.add
                                        ).then_inc(s["seg_sum_ready"], 1)
                scale_sums(now)
                dve.wait_ge(s["absent_ready"], t.k2)
                dve.wait_ge(s["seg_sum_ready"], t.k2)
                nc.vector.tensor_tensor(seg[:], seg_sum[:], wide(absent[:], 1, H), ALU.add).then_inc(s["seg_ready"], 1)
                dve.wait_ge(s["seg_ready"], t.k2)
                nc.vector.tensor_reduce(cands[:, :, 0], seg[:], AX.X, ALU.max)
                dve.wait_ge(s["spreadT_done"], t.k2)
                for j in range(2):
                    last = nc.vector.tensor_reduce(cands[:, :, 1 + j], bank[1 + j][0:NT, :].rearrange("d (h e) -> d h e", e=P),
                                                   AX.X, ALU.max)
                last.then_inc(s["cands_ready"], 1)
                dve.wait_ge(s["old_ready"], t.k2)
                dve.wait_ge(s["cands_ready"], t.k2)
                nc.vector.tensor_reduce(cands[:, :, NEW], cands[:, :, 0:NEW], AX.X, ALU.max).then_inc(s["newmax_ready"], 1)
                dve.wait_ge(s["newmax_ready"], t.k2)
                nc.vector.tensor_tensor(summed[:], cands[:, :, OLD:NEW + 1].rearrange("d h k -> d k h"),
                                        wide(self_row[t.u][:, HC + H:ROW], 1, 2), ALU.add).then_inc(s["sum_ready"], 1)
                dve.wait_ge(s["sum_ready"], t.k2)
                nc.vector.scalar_tensor_tensor(out=logit[:, 0:2, :], in0=summed[:], scalar=0.2, in1=summed[:],
                                               op0=ALU.mult, op1=ALU.max).then_inc(s["logit_ready"], 1)
                dve.wait_ge(s["logit_ready"], t.k2)
                dve.wait_ge(s["alpha_ready"], t.k2)
                nc.vector.tensor_copy(logit_p[:, 0], logit[:, 1:3, :]).then_inc(s["lpart0_ready"], 1)
                dve.wait_ge(s["scale_ready"], t.k1)
                nc.vector.tensor_tensor(fall[:], logit[:, 0, :], logit[:, 1, :], ALU.subtract).then_inc(s["fall_ready"], 1)
                dve.wait_ge(s["lpart0_ready"], t.k2)
                nc.vector.tensor_tensor(logit_r[:], logit[:, 1:3, :], logit_p[:, 0], ALU.subtract).then_inc(s["lrest_ready"], 1)
                dve.wait_ge(s["lrest_ready"], t.k2)
                nc.vector.tensor_copy(logit_p[:, 1], logit_r[:]).then_inc(s["lpart1_ready"], 1)
                dve.wait_ge(s["lpart1_ready"], t.k2)
                nc.vector.tensor_tensor(logit_p[:, 2], logit_r[:], logit_p[:, 1], ALU.subtract).then_inc(s["logit_parts_ready"], 1)

            def edge_logits(t):
                dve.wait_ge(s["edge_done"], t.k2)
                nc.vector.tensor_reduce(ev[:].rearrange("p t k h -> p t (k h)"),
                                        bank[1][:, 0:SLOTS * 6 * H].rearrange("p (t q a) -> p t a q", q=3, a=2 * H),
                                        AX.X, ALU.add).then_inc(s["ev_ready"], 1)
                dve.wait_ge(s["ev_ready"], t.k2)
                nc.vector.tensor_tensor(ye[:], G[t.u][:, :, HC:HC + H], ev[:, :, 1, :], ALU.add).then_inc(s["src_read"][t.u], 1)
                dve.wait_ge(s["src_read"][t.u], t.i + 2)
                nc.vector.scalar_tensor_tensor(out=ze[:], in0=ye[:], scalar=0.2, in1=ye[:], op0=ALU.mult, op1=ALU.max
                                               ).then_inc(s["z_ready"], 1)
                dve.wait_ge(s["z_ready"], t.k2)
                nc.vector.tensor_tensor(de[:], ze[:], ev[:, :, 0, :], ALU.subtract).then_inc(s["d_ready"], 1)
                dve.wait_ge(s["d_ready"], t.k2)
                nc.vector.tensor_scalar(ce[:], de[:], 0.0, None, ALU.min).then_inc(s["c_ready"], 1)

            def weigh(t, part):
                t0, t1 = PARTS[part]
                dve.wait_ge(s["w_ready"], t.k2)
                rows = G[t.u][:, t0:t1, 0:HC].rearrange("p t (h c) -> p t h c", h=H)
                nc.vector.tensor_tensor(rows, rows, wide(G[t.u][:, t0:t1, HC:HC + H], 3, C), ALU.mult
                                        ).then_inc(s["weighted"][part], 1)

            def scale_sums(t):
                if t:
                    dve.wait_ge(s["shares_ready"], t.k2)
                    dve.wait_ge(s["state_moved"], t.k1)
                    nc.vector.tensor_tensor(scaled[:, 0:HC].rearrange("d (h c) -> d h c", h=H),
                                            state[:, 0:HC].rearrange("d (h c) -> d h c", h=H), wide(keep[t.half][:], 2, C), ALU.mult)
                    nc.vector.tensor_tensor(scaled[:, HC:HC + H], state[:, HC:HC + H], keep[t.half][:], ALU.mult
                                            ).then_inc(s["scaled_ready"], 1)

            def mean_weight(t):
                if t:
                    dve.wait_ge(s["state_moved"], t.k2)
                    nc.vector.reciprocal(inv[:], state[:, HC:HC + H]).then_inc(s["inv_ready"], 1)

            def mean_product(t):
                if t:
                    dve.wait_ge(s["inv_ready"], t.k2)
                    dve.wait_ge(s["o_done"], t.k1)
                    nc.vector.tensor_tensor(mean_o[:].rearrange("d (h c) -> d h c", h=H),
                                            state[:, 0:HC].rearrange("d (h c) -> d h c", h=H), wide(inv[:], 2, C), ALU.mult
                                            ).then_inc(s["mean_ready"], 1)

            def residual(t):
                if t.L == 1:
                    dve.wait_ge(s["x2_landed"][t.u], t.r * 16 + 16)
                    dve.wait_ge(s["act_ready"], t.k2)
                    dve.wait_ge(stored, t.k * 16 + 16)
                    nc.vector.tensor_tensor(y_out[:], act_o[:], x_row[t.u][:], ALU.add).then_inc(s["x_read"][t.u], 1)

            def dve_start(t):
                onehots(t)
                run_maxima(t, None)
                tile_maxima(t, None)
                edge_logits(t)

            def dve_body(earlier, before, now, after):
                if after:
                    onehots(after)
                weigh(now, 0)
                if after:
                    run_maxima(after, before)
                else:
                    mean_weight(before)
                    mean_product(before)
                weigh(now, 1)
                weigh(now, 2)
                if after:
                    tile_maxima(after, now)
                else:
                    scale_sums(now)
                weigh(now, 3)
                if before:
                    residual(before)
                if after:
                    edge_logits(after)

            def dve_finish(earlier, t):
                mean_weight(t)
                mean_product(t)
                residual(t)

            pipeline(nc.vector, dve_start, dve_body, dve_finish)

        @block.tensor
        def _(pe):
            pe.wait_ge(const_ready, CONSTS)
            pe.wait_ge(w_landed, 32)
            for L in range(2):
                for k in range(KC):
                    for j in range(KC):
                        last = nc.tensor.transpose(bank[1 + L][:, k * D + j * P:k * D + (j + 1) * P],
                                                   w_in[:, L, j, k * P:(k + 1) * P], ident[:])
                last.then_inc(wT_done, 1)
            for u in range(2 * KC):
                pe.wait_ge(s["more_landed"][u], 16)
            pe.wait_ge(a_landed, 16 * 4 * H)
            pe.wait_ge(wT_copied, 2)
            for L in range(2):
                for j in range(KC):
                    for k in range(KC):
                        o0 = (L * KC + j) * 2 * H
                        last = nc.tensor.matmul(bank[0][:, o0:o0 + 2 * H], w_t[:, L, k, j * P:(j + 1) * P],
                                                a_blk[:, L, k, :], start=(k == 0), stop=(k == KC - 1))
            last.then_inc(wa_done, 1)
            pe.wait_ge(count_ready, 1)
            nc.tensor.matmul(bank[0][:, 256:256 + TILES + 1], ones[0:EP, :], count[:], start=True, stop=True).then_inc(rank_done, 1)
            pe.wait_ge(w_ext_ready, 1)
            pe.wait_ge(cast_ready, 1)

            def transpose_tile(g, t):
                k, r = t % 2, g.sizes[t]
                pe.wait_ge(hnT_copied[k], g.n * GROUP + g.b * GROUP // 2 + t // 2 + 1)
                pe.wait_ge(normed[g.b], g.n * GROUP + t + 1 + 1)
                for j in range(KC):
                    last = nc.tensor.transpose(bank[1 + k][:, j * P:j * P + r], hn[g.b][0:r, t, j * P:(j + 1) * P], ident[0:r, 0:r])
                last.then_inc(hnT_done[k], 1)

            def tile_rows(g, t):
                k, r = t % 2, g.sizes[t]
                if g.b == 0:
                    pe.wait_ge(rows_copied[1], g.n * GROUP + 1)
                else:
                    pe.wait_ge(rows_copied[0], g.n * GROUP + t + 1 + 1)
                pe.wait_ge(hnT_copied[k], g.n * GROUP + g.b * GROUP // 2 + t // 2 + 1 + 1)
                for j in range(KC):
                    last = nc.tensor.matmul(bank[3 + t][0:r, 0:ROW], hnT[k][:, j, 0:r], w_ext[:, 0, j, :],
                                            start=(j == 0), stop=(j == KC - 1))
                last.then_inc(rows_done[k], 1)

            def dense_group(g, after):
                for t in range(len(g.sizes)):
                    if t + 1 < len(g.sizes):
                        transpose_tile(g, t + 1)
                    elif after:
                        transpose_tile(after, 0)
                    tile_rows(g, t)

            transpose_tile(Group(0, 0), 0)
            with nc.tensor.Fori(0, TURNS) as i:
                for j in range(XB):
                    dense_group(Group(i, j), Group(i, j + 1))
            dense_group(Group(TURNS, 0), None)

            pe.wait_ge(fields_ready, 1)
            pe.wait_ge(rows_copied[0], GROUPS // 2 * GROUP + len(LAST) + 1)
            pe.wait_ge(rows_copied[1], GROUPS // 2 * GROUP + 1)
            for f in range(6):
                for j in range(2):
                    at = (f % 2) * STEPS + j * HALF_STEPS
                    last = nc.tensor.matmul(bank[f // 2][:, at:at + HALF_STEPS], field[:, f, j:j + 1].broadcast_to([HALF_STEPS, P]),
                                            ident[0:HALF_STEPS, 0:HALF_STEPS], start=True, stop=True)
            last.then_inc(fields_done, 1)
            pe.wait_ge(steps_ready, 1)

            def transpose_onehot(t):
                for f, r in enumerate(range(0, SLOTS, 8)):
                    pe.wait_ge(s["onehot_ready" if f else "onehot_lo_ready"], t.k2)
                    pe.wait_ge(s["onehotT_copied"][f % 2], t.k * (2 - f % 2) + f // 2 + 1)
                    to = bank[3 + f % 2][0:NT, :].bitcast(BF16)
                    for j in range(r, min(r + 8, SLOTS)):
                        last = nc.tensor.transpose(to[:, (j - r) * P:(j - r + 1) * P], onehot[:, j, :], ident_b[:])
                    last.then_inc(s["onehotT_done"][f % 2], 1)

            def runs_to_nodes(t):
                pe.wait_ge(s["marked_ready"], t.k2)
                w = 3 * H + 1
                for j in range(IN_RUN - 1):
                    last = nc.tensor.matmul(bank[0][0:NT, j * w:(j + 1) * w], onehot[:, j, :], marked[:, j, :], start=True, stop=True)
                last.then_inc(s["runs_done"], 1)

            def last_to_nodes(t):
                pe.wait_ge(s["spread_ready"], t.k2)
                for j in range(2):
                    for h in range(H):
                        last = nc.tensor.transpose(bank[1 + j][0:NT, h * P:(h + 1) * P], spread[:, j, h, :], ident[:])
                last.then_inc(s["spreadT_done"], 1)

            def logits_to_edges(t):
                pe.wait_ge(s["onehotT_copied"][0], t.k * 2 + 3)
                pe.wait_ge(s["onehotT_copied"][1], t.k2)
                pe.wait_ge(s["logit_parts_ready"], t.k2)
                w = 3 * 2 * H
                for j in range(SLOTS):
                    last = nc.tensor.matmul(bank[1][:, j * w:(j + 1) * w], onehotT[:, j, :],
                                            logit_p[:].rearrange("d q k h -> d (q k h)"), start=True, stop=True)
                last.then_inc(s["edge_done"], 1)

            def sum_up(t, part):
                t0, t1 = PARTS[part]
                if part == 0:
                    pe.wait_ge(s["onehot_f_ready"], t.k2)
                    pe.wait_ge(s["state_moved"], t.k1)
                pe.wait_ge(s["weighted"][part], t.k2)
                for j in range(t0, t1):
                    last = nc.tensor.matmul(bank[5][0:NT, 0:HC + H], onehot_f[t.half][:, j, :], G[t.u][:, j, 0:HC + H],
                                            start=(j == 0), stop=False)
                if part == len(PARTS) - 1:
                    pe.wait_ge(s["scaled_ready"], t.k2)
                    nc.tensor.matmul(bank[5][0:NT, 0:HC + H], ident[0:NT, 0:NT], scaled[:], start=False, stop=False)
                    pe.wait_ge(s["own_read"][t.u], t.i + 2)
                    nc.tensor.matmul(bank[5][0:NT, 0:HC + H], ident[0:NT, 0:NT], begin[t.half][:], start=False, stop=True
                                     ).then_inc(s["rows_used"][t.u], 1)

            def add_bias(t):
                pe.wait_ge(s["act_ready"], t.k1)
                pe.wait_ge(s["mean_ready"], t.k2)
                nc.tensor.matmul(bank[6][0:NT, O_AT:O_AT + HC], ident[0:NT, 0:NT], mean_o[:], start=True, stop=False)
                nc.tensor.matmul(bank[6][0:NT, O_AT:O_AT + HC], ones[0:1, 0:NT], b_row[0:1, t.L, :], start=False, stop=True
                                 ).then_inc(s["o_done"], 1)

            def transpose_act(t):
                if t.L == 0:
                    pe.wait_ge(s["act_ready"], t.k2)
                    for j in range(KC):
                        last = nc.tensor.transpose(bank[6][:, j * NT:(j + 1) * NT], act_o[:, j * P:(j + 1) * P], ident[0:NT, 0:NT])
                    last.then_inc(s["actT_done"], 1)

            def next_rows(t):
                if t.L == 0:
                    pe.wait_ge(s["row_copied"], t.k1)
                    pe.wait_ge(s["actT_copied"], t.k2)
                    for j in range(KC):
                        last = nc.tensor.matmul(bank[7][0:NT, 0:ROW], act_oT[:, j, :], w_ext[:, 1, j, :],
                                                start=(j == 0), stop=(j == KC - 1))
                    last.then_inc(s["row_done"], 1)

            def pe_start(t):
                transpose_onehot(t)
                runs_to_nodes(t)
                last_to_nodes(t)
                logits_to_edges(t)

            def pe_body(earlier, before, now, after):
                if after:
                    transpose_onehot(after)
                if earlier:
                    next_rows(earlier)
                sum_up(now, 0)
                if after:
                    runs_to_nodes(after)
                if before:
                    add_bias(before)
                if after:
                    last_to_nodes(after)
                sum_up(now, 1)
                sum_up(now, 2)
                if before:
                    transpose_act(before)
                if after:
                    logits_to_edges(after)
                sum_up(now, 3)

            def pe_finish(earlier, t):
                next_rows(earlier)
                add_bias(t)
                transpose_act(t)
                next_rows(t)

            pipeline(nc.tensor, pe_start, pe_body, pe_finish)


_INS = ["x", "src", "dst", "edge_attr_32", "L0_gnn_W0", "L0_gnn_a_src0", "L0_gnn_a_dst0", "L0_gnn_b0",
        "L0_gnn_W1", "L0_gnn_a_src1", "L0_gnn_a_dst1", "L0_gnn_b1"]
_OUTS = [((12500, 256), "float32")]


def kernel(**inputs):
    import numpy as _np
    import concourse.bacc as _bacc
    from concourse import mybir as _mybir
    from concourse.bass_utils import run_bass_kernel_spmd as _run

    nc = _bacc.Bacc("TRN2", target_bir_lowering=False, num_devices=1)
    arrays, args = {}, []
    for name in _INS:
        a = _np.ascontiguousarray(inputs[name])
        arrays[f"in_{name}_dram"] = a
        args.append(nc.dram_tensor(f"in_{name}_dram", a.shape, _mybir.dt.from_np(a.dtype), kind="ExternalInput").ap())
    for i, (shape, dtype) in enumerate(_OUTS):
        dt = _mybir.dt.from_np(_np.dtype(dtype))
        args.append(nc.dram_tensor(f"out_{i}_dram", shape, dt, kind="ExternalOutput").ap())
    two_layer_graph_attention(nc, *args)
    r = _run(nc, [arrays], core_ids=[0])
    got = tuple(r.results[0][f"out_{i}_dram"] for i in range(len(_OUTS)))
    return got[0]
```
